# Optimizing a Trainium2 kernel written in Bass

```python
import numpy as np
import jax
import jax.numpy as jnp

def _softmax(x, axis=-1):
    return jax.nn.softmax(x, axis=axis)

def _gelu(x):
    return jax.nn.gelu(x, approximate=True)

def _silu(x):
    return jax.nn.silu(x)

def _sigmoid(x):
    return jax.nn.sigmoid(x)

def _layernorm(x, axis=-1, eps=1e-05):
    m = jnp.mean(x, axis=axis, keepdims=True)
    v = jnp.var(x, axis=axis, keepdims=True)
    return (x - m) / jnp.sqrt(v + eps)

def _scatter_add(tgt, idx, src, axis=0):
    return tgt.at[idx].add(src)

def _segment_sum(src, seg, n):
    return jax.ops.segment_sum(src, seg, n)
kernel_name = 'mk_gnn_preln_d4_gnn_r16_098c9e'

def setup_inputs(seed: int=0):
    np.random.seed(seed)
    _w = jnp.asarray

    def _rec_inputs():
        import jax
        import jax.numpy as jnp
        _gk = jax.random.key(seed)
        x = -0.000202 + 1 * jax.random.normal(jax.random.fold_in(_gk, 1), (3125, 256), jnp.float32)
        _s = jax.random.randint(jax.random.fold_in(_gk, 2), (50000,), 0, 3125, jnp.int32)
        _d = jax.random.randint(jax.random.fold_in(_gk, 3), (50000,), 0, 3125, jnp.int32)
        _loop = jnp.arange(3125, dtype=jnp.int32)
        src = jnp.concatenate([_s, _d, _loop])
        dst = jnp.concatenate([_d, _s, _loop])
        _o = jnp.argsort(dst, stable=True)
        src = src[_o]
        dst = dst[_o]
        edge_weight = jax.random.uniform(jax.random.fold_in(_gk, 14), (103125,), jnp.float32, 0.0, 0.999999)
        return (x, src, dst, edge_weight)
    x, src, dst, edge_weight = _rec_inputs()

    def _L0_gnn_setup():
        import jax, jax.numpy as jnp
        import numpy as np
        N_NODES = 25000
        N_EDGES = 25000
        D = 256
        key = jax.random.key(seed)
        k1, k2, k3, k4, k5 = jax.random.split(key, 5)
        feat = jax.random.normal(k1, (N_NODES, D), dtype=jnp.float32)
        src = jax.random.randint(k2, (N_EDGES,), 0, N_NODES, dtype=jnp.int32)
        dst = jax.random.randint(k3, (N_EDGES,), 0, N_NODES, dtype=jnp.int32)
        a = float(np.sqrt(6.0 / (D + D)))
        W1 = jax.random.uniform(k4, (D, D), minval=-a, maxval=a, dtype=jnp.float32)
        W2 = jax.random.uniform(k5, (D, D), minval=-a, maxval=a, dtype=jnp.float32)
        b = jnp.zeros((D,), dtype=jnp.float32)
        return {'feat': feat, 'W1': W1, 'W2': W2, 'b': b, 'src': src, 'dst': dst}
    _L0_gnn_all = _L0_gnn_setup()
    _L0_gnn_in = {k: v for k, v in _L0_gnn_all.items() if k in ('W1', 'W2', 'b')}
    del _L0_gnn_all

    def _L1_gnn_setup():
        import jax, jax.numpy as jnp
        import numpy as np
        N_NODES = 6250
        N_EDGES = 100000
        D = 256
        key = jax.random.key(seed)
        ks = jax.random.split(key, 8)
        h6_all = jax.random.normal(ks[0], (N_NODES, D), dtype=jnp.float32)
        edge_index = jax.random.randint(ks[1], (2, N_EDGES), 0, N_NODES, dtype=jnp.int64)
        edge_weight = jax.random.uniform(ks[2], (N_EDGES,), dtype=jnp.float32)
        s = 1.0 / np.sqrt(D)
        W = jax.random.normal(ks[3], (D, D), dtype=jnp.float32) * s
        b = jnp.zeros((D,), dtype=jnp.float32)
        W1 = jax.random.normal(ks[4], (D, D), dtype=jnp.float32) * s
        b1 = jnp.zeros((D,), dtype=jnp.float32)
        W2 = jax.random.normal(ks[5], (D, D), dtype=jnp.float32) * s
        b2 = jnp.zeros((D,), dtype=jnp.float32)
        return {'h6_all': h6_all, 'edge_index': edge_index, 'edge_weight': edge_weight, 'W': W, 'b': b, 'W1': W1, 'b1': b1, 'W2': W2, 'b2': b2}
    _L1_gnn_all = _L1_gnn_setup()
    _L1_gnn_in = {k: v for k, v in _L1_gnn_all.items() if k in ('W', 'b', 'W1', 'b1', 'W2', 'b2')}
    del _L1_gnn_all

    def _L2_gnn_setup():
        import jax, jax.numpy as jnp
        import numpy as np
        V = 6250
        E = 18750
        D = 256
        BN_EPS = 1e-05
        key = jax.random.key(seed)
        ks = jax.random.split(key, 8)
        features = jax.random.normal(ks[0], (V, D), dtype=jnp.float32)
        edges = jax.random.randint(ks[1], (E, 2), 0, V, dtype=jnp.int64)
        s = 1.0 / np.sqrt(D)
        W0 = jax.random.normal(ks[2], (D, D), dtype=jnp.float32) * s
        b0 = jax.random.normal(ks[3], (D,), dtype=jnp.float32) * s
        W1 = jax.random.normal(ks[4], (D, D), dtype=jnp.float32) * s
        b1 = jax.random.normal(ks[5], (D,), dtype=jnp.float32) * s
        gamma = jnp.ones((D,), dtype=jnp.float32)
        beta = jnp.zeros((D,), dtype=jnp.float32)
        return {'features': features, 'edges': edges, 'W0': W0, 'b0': b0, 'W1': W1, 'b1': b1, 'gamma': gamma, 'beta': beta}
    _L2_gnn_all = _L2_gnn_setup()
    _L2_gnn_in = {k: v for k, v in _L2_gnn_all.items() if k in ('W0', 'b0', 'W1', 'b1', 'gamma', 'beta')}
    del _L2_gnn_all

    def _L3_gnn_setup():
        import jax, jax.numpy as jnp
        import numpy as np
        ALPHA = 0.2
        N_NODES = 3125
        N_EDGES = 50000
        IN_DIM = 256
        HEADS = 4
        OUT_DIM = 64
        key = jax.random.key(seed)
        k1, k2, k3, k4, k5, k6 = jax.random.split(key, 6)
        feat = jax.random.normal(k1, (N_NODES, IN_DIM), dtype=jnp.float32)
        src = jax.random.randint(k2, (N_EDGES,), 0, N_NODES, dtype=jnp.int32)
        dst = jax.random.randint(k3, (N_EDGES,), 0, N_NODES, dtype=jnp.int32)
        W = jax.random.normal(k4, (HEADS * OUT_DIM, IN_DIM), dtype=jnp.float32) * 0.05
        attn_l = jax.random.normal(k5, (HEADS, OUT_DIM), dtype=jnp.float32)
        attn_r = jax.random.normal(k6, (HEADS, OUT_DIM), dtype=jnp.float32)
        return {'feat': feat, 'src': src, 'dst': dst, 'W': W, 'attn_l': attn_l, 'attn_r': attn_r}
    _L3_gnn_all = _L3_gnn_setup()
    _L3_gnn_in = {k: v for k, v in _L3_gnn_all.items() if k in ('W', 'attn_l', 'attn_r')}
    del _L3_gnn_all
    return {'x': x, 'src': src, 'dst': dst, 'edge_weight': edge_weight, 'L0_gnn_W1': _L0_gnn_in['W1'], 'L0_gnn_W2': _L0_gnn_in['W2'], 'L0_gnn_b': _L0_gnn_in['b'], 'L1_gnn_W': _L1_gnn_in['W'], 'L1_gnn_b': _L1_gnn_in['b'], 'L1_gnn_W1': _L1_gnn_in['W1'], 'L1_gnn_b1': _L1_gnn_in['b1'], 'L1_gnn_W2': _L1_gnn_in['W2'], 'L1_gnn_b2': _L1_gnn_in['b2'], 'L2_gnn_W0': _L2_gnn_in['W0'], 'L2_gnn_b0': _L2_gnn_in['b0'], 'L2_gnn_W1': _L2_gnn_in['W1'], 'L2_gnn_b1': _L2_gnn_in['b1'], 'L2_gnn_gamma': _L2_gnn_in['gamma'], 'L2_gnn_beta': _L2_gnn_in['beta'], 'L3_gnn_W': _L3_gnn_in['W'], 'L3_gnn_attn_l': _L3_gnn_in['attn_l'], 'L3_gnn_attn_r': _L3_gnn_in['attn_r']}

def reference(x, src, dst, edge_weight, L0_gnn_W1, L0_gnn_W2, L0_gnn_b, L1_gnn_W, L1_gnn_b, L1_gnn_W1, L1_gnn_b1, L1_gnn_W2, L1_gnn_b2, L2_gnn_W0, L2_gnn_b0, L2_gnn_W1, L2_gnn_b1, L2_gnn_gamma, L2_gnn_beta, L3_gnn_W, L3_gnn_attn_l, L3_gnn_attn_r):
    import jax
    import jax.numpy as jnp

    def _L0_gnn_ref(feat, W1, W2, b, src, dst):
        import jax, jax.numpy as jnp
        import numpy as np
        N_NODES = 25000
        N_EDGES = 25000
        D = 256
        n = feat.shape[0]
        ones = jnp.ones(src.shape[0], dtype=feat.dtype)
        out_deg = jnp.maximum(jax.ops.segment_sum(ones, src, num_segments=n), 1.0)
        in_cnt = jax.ops.segment_sum(ones, dst, num_segments=n)
        t1 = feat @ W1
        msg = t1[src] + feat[src] * feat[dst] @ W2
        scale = jnp.sqrt(out_deg[src]) * jnp.sqrt(out_deg[dst])
        msg = msg / scale[:, None]
        agg = jax.ops.segment_sum(msg, dst, num_segments=n)
        embed = jnp.where(in_cnt[:, None] > 0, t1 + agg, jnp.zeros_like(t1))
        embed = embed + b
        embed = jax.nn.leaky_relu(embed, negative_slope=0.01)
        norm = jnp.linalg.norm(embed, axis=1, keepdims=True)
        embed = embed / jnp.maximum(norm, 1e-12)
        return embed

    def _L1_gnn_ref(h6_all, edge_index, edge_weight, W, b, W1, b1, W2, b2):
        import jax, jax.numpy as jnp
        import numpy as np
        N_NODES = 6250
        N_EDGES = 100000
        D = 256
        'GCNConv(256->256, weighted, self-loops, symmetric norm) + 2-layer MLP head.'
        N = h6_all.shape[0]
        row, col = (edge_index[0], edge_index[1])
        sl = jnp.arange(N, dtype=edge_index.dtype)
        row_sl = jnp.concatenate([row, sl])
        col_sl = jnp.concatenate([col, sl])
        ew_sl = jnp.concatenate([edge_weight, jnp.ones((N,), dtype=edge_weight.dtype)])
        deg = jax.ops.segment_sum(ew_sl, row_sl, num_segments=N)
        dinv = jnp.where(deg > 0, jax.lax.rsqrt(deg), 0.0)
        norm = dinv[row_sl] * ew_sl * dinv[col_sl]
        xw = h6_all @ W
        msgs = xw[col_sl] * norm[:, None]
        h7 = jax.ops.segment_sum(msgs, row_sl, num_segments=N) + b
        h = jax.nn.relu(h7 @ W1 + b1)
        out = h @ W2 + b2
        return out

    def _L2_gnn_ref(features, edges, W0, b0, W1, b1, gamma, beta):
        import jax, jax.numpy as jnp
        import numpy as np
        V = 6250
        E = 18750
        D = 256
        BN_EPS = 1e-05
        num_verts = features.shape[0]
        h_self = jnp.einsum('vd,od->vo', features, W0) + b0
        h_nbr = jnp.einsum('vd,od->vo', features, W1) + b1
        src = jnp.concatenate([edges[:, 0], edges[:, 1]])
        dst = jnp.concatenate([edges[:, 1], edges[:, 0]])
        agg = jax.ops.segment_sum(h_nbr[src], dst, num_segments=num_verts)
        y = h_self + agg
        mean = jnp.mean(y, axis=0)
        var = jnp.var(y, axis=0)
        y_hat = (y - mean) * jax.lax.rsqrt(var + BN_EPS) * gamma + beta
        return jax.nn.relu(y_hat)

    def _L3_gnn_ref(feat, src, dst, W, attn_l, attn_r):
        import jax, jax.numpy as jnp
        import numpy as np
        ALPHA = 0.2
        N_NODES = 3125
        N_EDGES = 50000
        IN_DIM = 256
        HEADS = 4
        OUT_DIM = 64
        n = feat.shape[0]
        ft = (feat @ W.T).reshape(n, HEADS, OUT_DIM)
        a1 = jnp.einsum('nhd,hd->nh', ft, attn_l)
        a2 = jnp.einsum('nhd,hd->nh', ft, attn_r)
        e = jax.nn.leaky_relu(a1[src] + a2[dst], negative_slope=ALPHA)
        m = jax.ops.segment_max(e, dst, num_segments=n)
        ex = jnp.exp(e - m[dst])
        s = jax.ops.segment_sum(ex, dst, num_segments=n)
        a = ex / s[dst]
        msg = ft[src] * a[:, :, None]
        out = jax.ops.segment_sum(msg, dst, num_segments=n)
        out = out.reshape(n, HEADS * OUT_DIM)
        return jax.nn.elu(out)
    edge_index = jnp.stack([src, dst])
    edge_index_t = jnp.stack([src, dst], axis=1)
    h = jnp.maximum(_layernorm(x, axis=-1), 0.0)
    x = x + _L0_gnn_ref(h, L0_gnn_W1, L0_gnn_W2, L0_gnn_b, src, dst)
    h = jnp.maximum(_layernorm(x, axis=-1), 0.0)
    x = x + _L1_gnn_ref(h, edge_index, edge_weight, L1_gnn_W, L1_gnn_b, L1_gnn_W1, L1_gnn_b1, L1_gnn_W2, L1_gnn_b2)
    h = jnp.maximum(_layernorm(x, axis=-1), 0.0)
    x = x + _L2_gnn_ref(h, edge_index_t, L2_gnn_W0, L2_gnn_b0, L2_gnn_W1, L2_gnn_b1, L2_gnn_gamma, L2_gnn_beta)
    h = jnp.maximum(_layernorm(x, axis=-1), 0.0)
    x = x + _L3_gnn_ref(h, src, dst, L3_gnn_W, L3_gnn_attn_l, L3_gnn_attn_r)
    return x

_drawn_inputs = setup_inputs


def setup_inputs(seed=0):
    import zlib

    import numpy as np

    out = dict(_drawn_inputs(seed))
    spreads = {'L0_gnn_b': (0.0, 0.8),
     'L1_gnn_b': (0.0, 0.1),
     'L1_gnn_b1': (0.0, 0.1),
     'L1_gnn_b2': (0.0, 0.1),
     'L2_gnn_gamma': (1.0, 0.2),
     'L2_gnn_beta': (0.0, 0.1)}
    factors = {'L0_gnn_W2': 2.954, 'L2_gnn_b0': 8.0}
    for name, (base, spread) in spreads.items():
        noise = np.random.default_rng([zlib.crc32(name.encode()), seed]).standard_normal(out[name].shape)
        drawn = base * np.exp(spread * noise) if base else spread * noise
        out[name] = jnp.asarray(drawn.astype(out[name].dtype))
    for name, factor in factors.items():
        out[name] = (out[name] * factor).astype(out[name].dtype)
    return out
```

```python
import concourse.bass as bass
from concourse import mybir
from contextlib import ExitStack

F32 = mybir.dt.float32
I32 = mybir.dt.int32
BF16 = mybir.dt.bfloat16
ALU = mybir.AluOpType
ACT = mybir.ActivationFunctionType
AX = mybir.AxisListType

P = 128
N = 3125
D = 256
NT = -(-N // P)
NP = NT * P
E = 103125
EC = -(-E // P)
EP = EC * P
HALF = EC // 2
SH = 64
W = EC + SH - 1
G = 13
NG = EC // G
GS = 26
NGS = EC // GS
assert NG * G == EC and NGS * GS == EC and 2 * HALF == EC
CELLS = NP * NP
KF = EP + EC
QB = -(-EC // P)
OUT_OF_TABLE = float(2 ** 24)
LN_EPS = 1e-5


def skewed(eng, n, main, late=None):
    late = late or (lambda k, s, r: None)
    main(0, 0, 0)
    with eng.Fori(0, (n - 1) // 2) as i:
        main(2 * i + 1, 1, i)
        late(2 * i, 0, i)
        main(2 * i + 2, 0, i + 1)
        late(2 * i + 1, 1, i)
    if n % 2 == 0:
        main(n - 1, 1, n // 2 - 1)
        late(n - 2, 0, n // 2 - 1)
        late(n - 1, 1, n // 2 - 1)
    else:
        late(n - 1, 0, n // 2)


def overlapped(eng, n, step):
    assert n % 2
    step((0, 0, 0), None)
    with eng.Fori(0, (n - 1) // 2) as i:
        step((2 * i + 1, 1, i), (2 * i, 0, i))
        step((2 * i + 2, 0, i + 1), (2 * i + 1, 1, i))
    step(None, (n - 1, 0, n // 2))


class Chain:

    def __init__(self, eng, sem):
        self.eng, self.sem, self.n, self.rounds = eng, sem, 0, 0

    def do(self, ins):
        self.n += 1
        ins.then_inc(self.sem, 1)

    def after(self):
        self.eng.wait_ge(self.sem, self.rounds + self.n)

    def run(self, n, per, tile):
        start = self.n

        def counted(k, s, r):
            self.n, self.rounds = start, k * per
            tile(k, s, r)
            assert self.n - start == per, self.n - start
        skewed(self.eng, n, counted)
        self.n, self.rounds = start + n * per, 0


class Shared:
    pass


def build(nc, x_in, src, dst, ew, iota, group, vecs, cols, w0, w1, w2, w3, out):
    ctx = ExitStack()
    sems = {}

    def sem(name):
        if name not in sems:
            sems[name] = ctx.enter_context(nc.semaphore(name))
        return sems[name]

    with ctx:
        def sb(name, shape, dt=F32, c=ctx):
            return c.enter_context(nc.sbuf_tensor(name, shape, dt))

        table = nc.dram_tensor("table", [CELLS, 2], F32)
        keyflat = nc.dram_tensor("keyflat", [KF + EP + KF], F32)
        ewflat = nc.dram_tensor("ewflat", [EP + KF], F32)
        turn = nc.dram_tensor("turn", [3, QB * P * P], F32)
        counts = nc.dram_tensor("counts", [NT, P, NT, P], F32)
        counts_t = nc.dram_tensor("counts_t", [NT, P, NT, P], F32)
        weights_t = nc.dram_tensor("weights_t", [NT, P, NT, P], F32)

        psum = ctx.enter_context(nc.psum_tensor("psum", [P, 8, 512], F32))
        xs = sb("xs", [P, NT, D])
        hx = sb("hx", [P, NT, D + 1])
        ident = sb("ident", [P, P])
        rso = sb("rso", [P, NT])
        dinv = sb("dinv", [P, NT])
        stats = sb("stats", [P, NT, 6])
        mv = sb("mv", [P, NT, 2])
        rstd = sb("rstd", [P, NT])
        shift = sb("shift", [P, NT])
        eps = sb("eps", [P, 1])

        def layernorm_stats(ch):
            eng = ch.eng
            for t in range(NT):
                ch.do(eng.bn_stats(stats[:, t, :], xs[:, t, :]))
            ch.after()

        def aggregate_stats(ch):
            for t in range(NT):
                ch.do(ch.eng.bn_aggr(mv[:, t, :], stats[:, t, :]))
            ch.after()

        def tile_stats(ch, k):
            one = lambda t: t[:, bass.ds(k, 1), :].rearrange("p a d -> p (a d)")
            ch.do(ch.eng.bn_stats(one(stats), one(xs)))

        def normalize(blk, scale=None):
            with ExitStack() as c:
                sd = sb(blk + "_sd", [P, NT], F32, c)
                rs, sh = sb(blk + "_rs", [P, NT], F32, c), sb(blk + "_sh", [P, NT], F32, c)
                block = c.enter_context(nc.Block())
                t = blk + "_ln_"

                @block.scalar
                def _(eng):
                    eng.wait_ge(sem(t + "mv"), 1)
                    eng.activation(sd[:, :], mv[:, :, 1], ACT.Sqrt, bias=eps[:, :]).then_inc(sem(t + "sd"), 1)
                    eng.wait_ge(sem(t + "shift"), 1)
                    for i in range(NT):
                        eng.activation(hx[:, i, 0:D], xs[:, i, :], ACT.Relu, bias=sh[:, i:i + 1], scale=rs[:, i:i + 1])

                @block.vector
                def _(eng):
                    ch = Chain(eng, sem(t + "dve"))
                    aggregate_stats(ch)
                    eng.sem_inc(sem(t + "mv"), 1)
                    eng.wait_ge(sem(t + "sd"), 1)
                    ch.do(eng.reciprocal(rs[:, :], sd[:, :]))
                    ch.after()
                    if scale is not None:
                        ch.do(eng.tensor_tensor(rs[:, :], rs[:, :], scale[:, :], ALU.mult))
                        ch.after()
                    ch.do(eng.scalar_tensor_tensor(out=sh[:, :], in0=mv[:, :, 0], scalar=-1.0, in1=rs[:, :],
                                                   op0=ALU.mult, op1=ALU.mult))
                    ch.after()
                    eng.sem_inc(sem(t + "shift"), 1)

        shared = Shared()
        shared.x_in, shared.src, shared.dst = x_in, src, dst
        shared.ew, shared.iota, shared.group = ew, iota, group
        shared.vecs, shared.cols, shared.w0 = vecs, cols, w0
        shared.w1, shared.w2, shared.w3 = w1, w2, w3
        shared.table, shared.keyflat, shared.ewflat = table, keyflat, ewflat
        shared.turn, shared.counts, shared.counts_t = turn, counts, counts_t
        shared.weights_t, shared.psum, shared.xs = weights_t, psum, xs
        shared.hx, shared.ident, shared.rso = hx, ident, rso
        shared.dinv, shared.rstd, shared.shift = dinv, rstd, shift
        shared.mv, shared.eps, shared.layernorm_stats = mv, eps, layernorm_stats
        shared.aggregate_stats, shared.tile_stats = aggregate_stats, tile_stats
        phase_edges_and_l0(nc, sem, sb, shared)
        normalize("l1", dinv)
        phase_l1(nc, sem, sb, shared)
        normalize("l2")
        phase_l2(nc, sem, sb, shared)
        normalize("l3")
        phase_l3(nc, sem, sb, shared)
        block = nc.Block()
        with block as b:
            @b.sync
            def _(eng):
                eng.dma_start(out[0:24 * P, :].rearrange("(t p) d -> p t d", p=P), xs[:, 0:24, :]).then_inc(sem("out"), 16)
                eng.dma_start(out[24 * P:N, :], xs[0:N - 24 * P, 24, :]).then_inc(sem("out"), 16)
                eng.wait_ge(sem("out"), 32)


def phase_edges_and_l0(nc, sem, sb, a):
    psum, xs, hx, ident, rso, dinv = a.psum, a.xs, a.hx, a.ident, a.rso, a.dinv
    rstd, shift, mv, eps = a.rstd, a.shift, a.mv, a.eps
    table, keyflat, ewflat, turn = a.table.ap(), a.keyflat.ap(), a.ewflat.ap(), a.turn.ap()
    counts, counts_t, weights_t = a.counts.ap(), a.counts_t.ap(), a.weights_t.ap()
    ctx = ExitStack()
    with ctx:
        def buf(name, shape, dt=F32):
            return sb(name, shape, dt, ctx)
        tk = buf("tk", [P, 2, NT, P, 2])
        zero = tk[:, 1, :, :, :].rearrange("p j d c -> p (j d c)")
        region = buf("region", [P, 3, NP])
        cs = region[:, 0, :].rearrange("p (j d) -> p j d", j=NT)
        ct = region[:, 1, :].rearrange("p (j s) -> p j s", j=NT)
        wt = region[:, 2, :].rearrange("p (j s) -> p j s", j=NT)
        flat = region[:, :, :].rearrange("p a n -> p (a n)")

        def f(n, width=EC):
            return flat[:, n * EC:n * EC + width]
        srci, dsti, dst1, dst2, dst3, t0, t1 = (f(n).bitcast(I32) for n in range(7))
        f0, f1, key, sent = (f(n) for n in range(7, 11))
        lo, hi, cnt_e, w_e, idx_e = f(3), f(4), f(5), f(6), f(8)
        two = buf("two", [P, 5900])
        keyF, keyB, ewF = (two[:, n * W:(n + 1) * W] for n in range(3))
        eqF, eqB = (two[:, 3 * W + n * EC:3 * W + (n + 1) * EC].bitcast(BF16).rearrange("p (s c) -> p s c", s=2) for n in range(2))
        wF = two[:, 3 * W + 2 * EC:3 * W + 4 * EC].rearrange("p (s c) -> p s c", s=2)
        hlo = two[:, 0:2 * G * P].rearrange("p (s c n) -> p s c n", s=2, c=G)
        hhi = two[:, 2 * G * P:2 * G * P + 4 * G * NT].rearrange("p (s c a n) -> p s c a n", s=2, c=G, a=2)
        ewt = buf("ewt", [P, EC])
        gno = buf("gno", [P, EC])
        rl = tk[:, 0, :, :, :].rearrange("p j d c -> p (j d c)")[:, 0:3 * QB * P].rearrange("p (a q e) -> p a q e", a=3, q=QB)
        bc = buf("bc", [P, 1, D])
        idxT = buf("idxT", [P, EC], I32)
        valT = buf("valT", [P, EC, 2])
        idxs = buf("idxs", [P, 2, GS], I32)
        vals = buf("vals", [P, 2, GS, 2])
        io = buf("io", [P, P])
        identb = buf("identb", [P, P], BF16)
        zbb = buf("zbb", [P, 512], BF16)
        st = buf("st", [P, 8])
        sti = buf("sti", [P, 4], I32)
        gm = buf("gm", [P, NT])
        gmax = buf("gmax", [NT, 1])
        need = buf("need", [1, NT], I32)
        wl0 = buf("wl0", [P, 4, D])
        hk = buf("hk", [P, D])
        q = buf("q", [P, D])
        ab = buf("ab", [P, 2, D])
        abT = buf("abT", [P, 4, P])
        e1 = buf("e1", [P, D])
        e2 = buf("e2", [P, D])
        sq = buf("sq", [P, D])
        msk = buf("msk", [P, 1])
        nrm = buf("nrm", [P, 4])
        od2 = buf("od2", [P, 2, NT])
        od3 = buf("od3", [P, 2, NT])
        pc, pd, pw = psum[:, 0:2, :], psum[:, 2:4, :], psum[:, 4:6, :]
        ph = psum[:, 6, 0:2 * NT]
        pg = psum[:, 7, :]
        pq = psum[:, 0:2, :]
        ptc, ptw = psum[:, 2:4, :], psum[:, 4:6, :]
        pab, pe = psum[:, 6, :], psum[:, 7, 0:D]

        def shifts(eng):
            eng.wait_ge(sem("shift"), 1)
            blocks = eng.value_load(sti[0:1, 1:2], min_val=1, max_val=EP // SH + 1)
            inner = eng.value_load(sti[0:1, 2:3], min_val=1, max_val=SH // 2)
            return blocks, inner

        block = ctx.enter_context(nc.Block())

        @block.sync
        def _(eng):
            rows = lambda t: t.rearrange("(p c) -> p c", p=P)
            for t, s in ((srci, a.src[0:EP]), (dsti, a.dst[0:EP]), (dst1, a.dst[1:EP + 1]),
                         (dst2, a.dst[HALF:HALF + EP]), (dst3, a.dst[HALF + 1:HALF + 1 + EP]), (ewt[:, :], a.ew)):
                eng.dma_start(t, rows(s)).then_inc(sem("ld"), 16)
            eng.dma_start(io[:, :], a.iota).then_inc(sem("ld2"), 16)
            eng.dma_start(gno[:, :], a.group).then_inc(sem("ld2"), 16)
            eng.dma_start(xs[:, 0:NT - 1, :], a.x_in[0:(NT - 1) * P, :].rearrange("(t p) d -> p t d", p=P)).then_inc(sem("ldx"), 16)
            eng.wait_ge(sem("xpad"), 1)
            eng.dma_start(xs[0:N - (NT - 1) * P, NT - 1, :], a.x_in[(NT - 1) * P:N, :]).then_inc(sem("ldx"), 16)
            eng.dma_start(wl0[:, :, :], a.w0.rearrange("(c p) o -> p c o", p=P)).then_inc(sem("ld3"), 16)
            eng.dma_start(bc[:, 0, :], a.vecs[0:1, :].to_broadcast([P, D])).then_inc(sem("ld3"), 16)
            eng.wait_ge(sem("zero"), 1)
            eng.wait_ge(sem("win"), 48)
            tz = table.rearrange("(k p c) w -> k p (c w)", k=NT, p=P)

            def clear(k, s, r):
                if not isinstance(k, int):
                    eng.wait_ge(sem(f"ztab{1 - s}"), 16 * (r + 1 if s else r))
                eng.dma_start(tz[bass.ds(k, 1), :, :].rearrange("a p c -> (a p) c"), zero).then_inc(sem(f"ztab{s}"), 16)
            skewed(eng, NT, clear)
            eng.wait_ge(sem("ztab0"), 16 * (NT - NT // 2))
            eng.wait_ge(sem("ztab1"), 16 * (NT // 2))
            eng.sem_inc(sem("tabz"), 1)
            eng.wait_ge(sem("need"), 1)

            def load(k, s, r):
                eng.wait_ge(sem("tv"), 7 * k + 7)
                eng.wait_ge(sem("ta"), 7 * k + 7)
                if isinstance(k, int):
                    n = eng.value_load(need[0:1, k:k + 1], min_val=1, max_val=NGS)
                else:
                    n = eng.value_load(need[0:1, bass.ds(k, 1)], min_val=1, max_val=NGS)
                eng.wait_ge(sem("done"), n)
                eng.sem_inc(sem("pass"), 1)
                src_ap = tz[bass.ds(k, 1), :, :].rearrange("a p c -> (a p) c")
                eng.dma_start(tk[:, s, :, :, :].rearrange("p j d c -> p (j d c)"), src_ap).then_inc(sem(f"tk{s}"), 16)

            def store(k, s, r):
                one = lambda t: t[bass.ds(k, 1), :, :, :].rearrange("a p j d -> (a p) j d")
                eng.wait_ge(sem("cs"), k + 1)
                eng.dma_start(one(counts), cs).then_inc(sem("cs_out"), 16)
                col = lambda t: t[:, :, bass.ds(k, 1), :].rearrange("j p k s -> p (j k) s")
                eng.wait_ge(sem("tv"), 14 + 7 * k + 7)
                eng.dma_start(col(counts_t), ct).then_inc(sem("ct_out"), 16)
                eng.wait_ge(sem("ta"), 14 + 7 * k + 7)
                eng.dma_start(col(weights_t), wt).then_inc(sem("wt_out"), 16)
            skewed(eng, NT, load, store)
            for n in ("cs_out", "ct_out", "wt_out"):
                eng.wait_ge(sem(n), 16 * NT)

        @block.gpsimd
        def _(eng):
            n = [0]

            def do(ins):
                n[0] += 1
                ins.then_inc(sem("pool"), 1)
            eng.memset(zero, 0.0).then_inc(sem("zero"), 1)
            do(eng.memset(ident[:, :], 0.0))
            do(eng.memset(zbb[:, :], 0.0))
            do(eng.memset(sent, -1.0))
            do(eng.memset(eps[:, :], LN_EPS))
            do(eng.memset(rl[:, :, QB - 1, :], 0.0))
            do(eng.memset(hx[:, :, D:D + 1], 1.0))
            eng.memset(xs[:, NT - 1, :], 0.0).then_inc(sem("xpad"), 1)
            eng.wait_ge(sem("pool"), n[0])
            do(eng.affine_select(out=ident[:, :], in_=ident[:, :], compare_op=ALU.not_equal, fill=1.0,
                                 base=0, pattern=[[-1, P]], channel_multiplier=1))
            eng.wait_ge(sem("pool"), n[0])
            eng.tensor_copy(identb[:, :], ident[:, :]).then_inc(sem("const"), 1)
            eng.wait_ge(sem("turned"), 1)
            eng.wait_ge(sem("tabz"), 1)

            def issue(g, s, r):
                eng.tensor_copy(idxs[:, s, :], idxT[:, bass.ds(GS * g, GS)]).then_inc(sem("stage"), 1)
                eng.tensor_copy(vals[:, s, :, :], valT[:, bass.ds(GS * g, GS), :]).then_inc(sem("stage"), 1)
                eng.wait_ge(sem("stage"), 2 * g + 2)
                eng.sem_inc(sem("pass_p"), 1)
                for c in range(GS):
                    eng.indirect_dma_start(out=table, out_offset=bass.IndirectOffsetOnAxis(idxs[:, s, c:c + 1], 0),
                                           in_=vals[:, s, c, :], in_offset=None, bounds_check=CELLS - 1,
                                           oob_is_err=False).then_inc(sem(f"scat{s}"), 16)

            def finish(g, s, r):
                eng.wait_ge(sem(f"scat{s}"), 16 * GS * (r + 1))
                eng.sem_inc(sem("done"), 1)
            skewed(eng, NGS, issue, finish)

        @block.vector
        def _(eng):
            ch = Chain(eng, sem("dve"))
            do, after = ch.do, ch.after
            eng.wait_ge(sem("ld"), 96)
            do(eng.tensor_scalar(t0, dsti, 7, None, ALU.logical_shift_right))
            do(eng.tensor_scalar(t1, dsti, 127, None, ALU.bitwise_and))
            after()
            do(eng.scalar_tensor_tensor(out=f0, in0=t0, scalar=float(P * NP), in1=t1, op0=ALU.mult, op1=ALU.add))
            after()
            do(eng.tensor_scalar(t0, srci, 7, None, ALU.logical_shift_right))
            do(eng.tensor_scalar(t1, srci, 127, None, ALU.bitwise_and))
            after()
            do(eng.scalar_tensor_tensor(out=f1, in0=t0, scalar=float(P), in1=f0, op0=ALU.mult, op1=ALU.add))
            after()
            do(eng.scalar_tensor_tensor(out=key, in0=t1, scalar=float(NP), in1=f1, op0=ALU.mult, op1=ALU.add))
            after()
            eng.wait_ge(sem("const"), 1)
            eng.sem_inc(sem("key"), 1)
            do(eng.tensor_tensor(f0, dsti, dst1, ALU.is_gt))
            after()
            do(eng.tensor_reduce(st[:, 0:1], f0, AX.X, ALU.max))
            do(eng.tensor_tensor(f1, dsti, dst1, ALU.is_equal))
            after()
            do(eng.tensor_tensor_scan(f0, f1, f1, 0.0, ALU.mult, ALU.add))
            after()
            do(eng.tensor_reduce(st[:, 1:2], f0, AX.X, ALU.max))
            do(eng.tensor_tensor(f1, dst2, dst3, ALU.is_equal))
            after()
            do(eng.tensor_tensor_scan(f0, f1, f1, 0.0, ALU.mult, ALU.add))
            after()
            do(eng.tensor_reduce(st[:, 2:3], f0, AX.X, ALU.max))
            after()
            do(eng.tensor_tensor(st[:, 3:4], st[:, 1:2], st[:, 2:3], ALU.max))
            after()
            do(eng.tensor_scalar(st[:, 6:7], st[:, 3:4], float(HALF - 1), None, ALU.is_ge))
            after()
            do(eng.tensor_tensor(st[:, 7:8], st[:, 6:7], st[:, 0:1], ALU.max))
            after()
            do(eng.scalar_tensor_tensor(out=st[:, 4:5], in0=st[:, 7:8], scalar=float(EP), in1=st[:, 3:4],
                                        op0=ALU.mult, op1=ALU.max))
            after()
            eng.sem_inc(sem("run"), 1)
            eng.wait_ge(sem("run_t"), 1)
            do(eng.tensor_reduce(st[0:1, 5:6], pg[0:1, 0:P], AX.X, ALU.max))
            after()
            do(eng.tensor_scalar(sti[0:1, 0:1], st[0:1, 5:6], 1.0, None, ALU.max))
            after()
            do(eng.tensor_scalar(sti[0:1, 1:2], sti[0:1, 0:1], float(SH - 1), None, ALU.add))
            do(eng.tensor_scalar(sti[0:1, 2:3], sti[0:1, 0:1], 1.0, float(SH), ALU.add, ALU.min))
            after()
            do(eng.tensor_scalar(sti[0:1, 1:2], sti[0:1, 1:2], 6, None, ALU.logical_shift_right))
            do(eng.tensor_scalar(sti[0:1, 2:3], sti[0:1, 2:3], 1, None, ALU.logical_shift_right))
            after()
            eng.sem_inc(sem("shift"), 1)
            eng.sem_inc(sem("winfree"), 1)
            blocks, inner = shifts(eng)
            with eng.Fori(0, blocks) as b:
                with eng.Fori(0, inner) as i:
                    for s in range(2):
                        jj = 2 * i + s
                        eng.wait_ge(sem("win"), 48 * b + 48)
                        eng.wait_ge(sem("eqfree"), 2 * (b * inner + i) + s + 1)
                        eng.tensor_tensor(eqF[:, s, :], key, keyF[:, bass.ds(jj, EC)], ALU.is_equal).then_inc(sem("eqF"), 1)
                        eng.tensor_tensor(eqB[:, s, :], key, keyB[:, bass.ds(SH - 1 - jj, EC)], ALU.is_equal).then_inc(sem("eq"), 1)
                        eng.wait_ge(sem("eqF"), (b * inner + i) * 2 + s + 1)
                        eng.tensor_tensor(wF[:, s, :], eqF[:, s, :], ewF[:, bass.ds(jj, EC)], ALU.mult).then_inc(sem("eq"), 1)
                eng.drain()
                eng.sem_inc(sem("winfree"), 1)
            eng.wait_ge(sem("sums"), 1)
            pv = lambda p: p[:, :, 0:HALF]
            hv = lambda t: t.rearrange("p (a c) -> p a c", a=2)
            do(eng.tensor_scalar(hv(cnt_e), pv(pc), 1.0, None, ALU.add))
            do(eng.tensor_tensor(hv(w_e), pv(pw), hv(ewt[:, :]), ALU.add))
            do(eng.tensor_scalar(hv(f0), pv(pd), 1.0, OUT_OF_TABLE, ALU.min, ALU.mult))
            after()
            do(eng.tensor_tensor(idx_e, f0, key, ALU.add))
            after()
            eng.sem_inc(sem("edges"), 1)
            do(eng.tensor_scalar(dst1, srci, 127, None, ALU.bitwise_and))
            do(eng.tensor_scalar(dsti, dsti, 7, None, ALU.logical_shift_right))
            do(eng.tensor_scalar(srci, srci, 7, None, ALU.logical_shift_right))
            after()
            do(eng.tensor_copy(lo, dst1))
            do(eng.tensor_copy(hi, srci))
            do(eng.tensor_copy(key, dsti))
            after()
            eng.wait_ge(sem("cols"), 1)
            for a0, b0, src_bank in ((0, 512, 0), (512, EC, 1)):
                w = b0 - a0
                do(eng.tensor_copy(idxT[:, a0:b0], pc[:, src_bank, 0:w]))
                do(eng.tensor_copy(valT[:, a0:b0, 0], pd[:, src_bank, 0:w]))
                do(eng.tensor_copy(valT[:, a0:b0, 1], pw[:, src_bank, 0:w]))
            after()
            eng.sem_inc(sem("turned"), 1)
            eng.wait_ge(sem("ld2"), 32)
            for k in range(NT):
                fs = (f0, f1)[k % 2]
                do(eng.scalar_tensor_tensor(out=fs, in0=key, scalar=float(k), in1=gno[:, :], op0=ALU.is_equal, op1=ALU.mult))
                after()
                do(eng.tensor_reduce(gm[:, k:k + 1], fs, AX.X, ALU.max))
            after()
            eng.sem_inc(sem("gm"), 1)
            eng.wait_ge(sem("gm_t"), 1)
            do(eng.tensor_reduce(gmax[:, :], pg[0:NT, 0:P], AX.X, ALU.max))
            after()
            do(eng.tensor_scalar(gmax[:, :], gmax[:, :], 1.0, None, ALU.max))
            after()
            eng.sem_inc(sem("gmax"), 1)
            eng.wait_ge(sem("gmax_t"), 1)
            do(eng.tensor_copy(need[:, :], pg[0:1, 256:256 + NT]))
            after()
            eng.sem_inc(sem("need"), 1)

            def onehot(g, s, r):
                cols = lambda t: t[:, bass.ds(G * g, G)].unsqueeze(2)
                if not (isinstance(g, int) and g == 0):
                    eng.wait_ge(sem("hfree"), g)
                eng.tensor_tensor(hlo[:, s, :, :], cols(lo).to_broadcast([P, G, P]),
                                  io[:, :].unsqueeze(1).to_broadcast([P, G, P]), ALU.is_equal).then_inc(sem("hot"), 1)
                do(eng.tensor_tensor(hhi[:, s, :, 0, :], cols(hi).to_broadcast([P, G, NT]),
                                     io[:, 0:NT].unsqueeze(1).to_broadcast([P, G, NT]), ALU.is_equal))
                after()
                eng.tensor_tensor(hhi[:, s, :, 1, :], hhi[:, s, :, 0, :],
                                  cols(ewt[:, :]).to_broadcast([P, G, NT]), ALU.mult).then_inc(sem("hot"), 1)
            ch.run(NG, 1, onehot)
            eng.wait_ge(sem("ldx"), 32)
            a.layernorm_stats(ch)
            a.aggregate_stats(ch)
            eng.wait_ge(sem("deg"), 1)
            php = ph.rearrange("p (a n) -> p a n", a=2)
            do(eng.tensor_scalar(od2[:, 0, :], php[:, 0, :], 1.0, None, ALU.max))
            do(eng.tensor_scalar(od3[:, 1, :], php[:, 1, :], 1.0, None, ALU.add))
            after()
            do(eng.tensor_scalar(od2[:, 1, :], od3[:, 1, :], 1e-30, None, ALU.max))
            after()
            eng.sem_inc(sem("stat"), 1)
            eng.wait_ge(sem("stat_r"), 1)
            do(eng.reciprocal(rso[:, :], od3[:, 0, :]))
            do(eng.tensor_scalar(gm[:, :], od2[:, 1, :], 1e-30, None, ALU.is_gt))
            do(eng.reciprocal(dinv[:, :], od2[:, 0, :]))
            do(eng.reciprocal(rstd[:, :], shift[:, :]))
            after()
            do(eng.tensor_tensor(dinv[:, :], dinv[:, :], gm[:, :], ALU.mult))
            do(eng.scalar_tensor_tensor(out=shift[:, :], in0=mv[:, :, 0], scalar=-1.0, in1=rstd[:, :], op0=ALU.mult, op1=ALU.mult))
            after()
            do(eng.tensor_tensor(od3[:, 0, :], rstd[:, :], rso[:, :], ALU.mult))
            do(eng.tensor_tensor(od3[:, 1, :], shift[:, :], rso[:, :], ALU.mult))
            after()
            eng.sem_inc(sem("scaled"), 1)
            eng.wait_ge(sem("ld3"), 32)
            eng.sem_inc(sem("tv"), 14)
            eng.sem_inc(sem("ab"), 2)

            def tile(k, s, r):
                one = lambda t: t[:, bass.ds(k, 1)]
                eng.wait_ge(sem("q"), k + 1)
                eng.wait_ge(sem("abfree"), k + 1)
                do(eng.tensor_scalar(q[:, :], pq[:, s, 0:D], one(rso), None, ALU.mult))
                do(eng.tensor_scalar(msk[:, :], pq[:, s, D:D + 1], 0.0, None, ALU.is_gt))
                after()
                eng.wait_ge(sem("hk"), k + 1)
                do(eng.tensor_tensor(ab[:, 0, :], q[:, :], hk[:, :], ALU.add))
                after()
                eng.tensor_tensor(ab[:, 1, :], q[:, :], hk[:, :], ALU.mult).then_inc(sem("ab"), 1)
                for g in range(7):
                    w = min(4, NT - 4 * g)
                    eng.wait_ge(sem("tc"), 7 * k + g + 1)
                    if g == 0 and not (isinstance(k, int)):
                        eng.wait_ge(sem("ct_out"), 16 * k)
                    eng.tensor_copy(ct[:, 4 * g:4 * g + w, :].rearrange("p j s -> p (j s)"),
                                    ptc[:, (g + s) % 2, 0:w * P]).then_inc(sem("tv"), 1)
                eng.wait_ge(sem("e"), k + 1)
                do(eng.scalar_tensor_tensor(out=e1[:, :], in0=pe, scalar=msk[:, :], in1=bc[:, 0, :], op0=ALU.mult, op1=ALU.add))
                after()
                do(eng.scalar_tensor_tensor(out=e2[:, :], in0=e1[:, :], scalar=0.01, in1=e1[:, :], op0=ALU.mult, op1=ALU.max))
                after()
                eng.tensor_tensor_reduce(out=sq[:, :], in0=e2[:, :], in1=e2[:, :], scale=1.0, scalar=0.0,
                                         op0=ALU.mult, op1=ALU.add, accum_out=nrm[:, 0:1]).then_inc(sem("ss"), 1)
                eng.wait_ge(sem("root"), k + 1)
                do(eng.tensor_scalar(nrm[:, 2:3], nrm[:, 1:2], 1e-12, None, ALU.max))
                after()
                do(eng.reciprocal(nrm[:, 3:4], nrm[:, 2:3]))
                after()
                xk = xs[:, bass.ds(k, 1), :].rearrange("p a d -> p (a d)")
                do(eng.scalar_tensor_tensor(out=xk, in0=e2[:, :], scalar=nrm[:, 3:4], in1=xk, op0=ALU.mult, op1=ALU.add))
                after()
                a.tile_stats(ch, k)
            ch.run(NT, 9, tile)

        @block.scalar
        def _(eng):
            kf = lambda t: t.rearrange("(p c) -> p c", p=P)
            row = lambda t: t.rearrange("(p c) -> p c", p=1)
            eng.wait_ge(sem("const"), 1)
            eng.wait_ge(sem("ld"), 96)
            for d, t in ((keyflat[0:EP], sent), (keyflat[KF + EP:KF + 2 * EP], sent),
                         (ewflat[0:EP], ewt[:, :]), (ewflat[EP:2 * EP], sent)):
                eng.dma_start(kf(d), t).then_inc(sem("flat"), 16)
            for d in (keyflat[EP:KF], keyflat[KF + 2 * EP:2 * KF + EP], ewflat[2 * EP:EP + KF]):
                eng.dma_start(row(d), sent[0:1, :]).then_inc(sem("flat"), 16)
            eng.wait_ge(sem("key"), 1)
            eng.dma_start(kf(keyflat[KF:KF + EP]), key).then_inc(sem("flat"), 16)
            eng.wait_ge(sem("flat"), 128)
            blocks, inner = shifts(eng)
            with eng.Fori(0, blocks) as b:
                eng.wait_ge(sem("winfree"), b + 1)

                def window(t, off):
                    base = t[bass.ds(off, EP)].rearrange("(p c) -> p c", p=P)
                    return bass.AP(tensor=base.tensor, offset=base.offset, ap=[[EC, P], [1, W]])
                for tile, t, off in ((keyF, keyflat, KF + 1 + SH * b), (keyB, keyflat, KF - SH - SH * b),
                                     (ewF, ewflat, 1 + SH * b)):
                    eng.dma_start(tile, window(t, off)).then_inc(sem("win"), 16)
            eng.wait_ge(sem("edges"), 1)
            for n, t in enumerate((idx_e, cnt_e, w_e)):
                eng.dma_start(kf(turn[n, 0:EP]), t).then_inc(sem("turn_out"), 16)
            eng.wait_ge(sem("turn_out"), 48)
            for n in range(3):
                eng.dma_start(rl[:, n, 0:QB - 1, :], turn[n, 0:(QB - 1) * P * P].rearrange("(b q e) -> q b e", q=P, e=P)).then_inc(sem("turn_in"), 16)
                rest = EC - (QB - 1) * P
                eng.dma_start(rl[0:rest, n, QB - 1, :], turn[n, (QB - 1) * P * P:EP].rearrange("(q e) -> q e", e=P)).then_inc(sem("turn_in"), 16)
            eng.wait_ge(sem("stat"), 1)
            eng.activation(od3[:, 0, :], od2[:, 0, :], ACT.Sqrt).then_inc(sem("act"), 1)
            eng.activation(shift[:, :], mv[:, :, 1], ACT.Sqrt, bias=eps[:, :]).then_inc(sem("act"), 1)
            eng.wait_ge(sem("act"), 2)
            eng.activation(od2[:, 0, :], od2[:, 1, :], ACT.Sqrt).then_inc(sem("stat_r"), 1)
            eng.wait_ge(sem("scaled"), 1)
            for t in range(NT):
                last = eng.activation(hx[:, t, 0:D], xs[:, t, :], ACT.Relu, bias=od3[:, 1, t:t + 1], scale=od3[:, 0, t:t + 1])
            last.then_inc(sem("u"), 1)
            eng.sem_inc(sem("ta"), 14)
            eng.sem_inc(sem("abfree"), 1)

            def tile(k, s, r):
                one = lambda t: t[:, bass.ds(k, 1)]
                eng.wait_ge(sem(f"tk{s}"), 16 * r + 16)
                if not isinstance(k, int):
                    eng.wait_ge(sem("cs_out"), 16 * k)
                eng.activation(cs, tk[:, s, :, :, 0], ACT.Copy).then_inc(sem("cs"), 1)
                eng.wait_ge(sem("ab"), k + 2)
                eng.activation(hk[:, :], xs[:, bass.ds(k, 1), :].rearrange("p a d -> p (a d)"), ACT.Relu,
                               bias=one(shift), scale=one(rstd)).then_inc(sem("hk"), 1)
                for g in range(7):
                    w = min(4, NT - 4 * g)
                    eng.wait_ge(sem("tw"), 7 * k + g + 1)
                    if g == 0 and not isinstance(k, int):
                        eng.wait_ge(sem("wt_out"), 16 * k)
                    eng.activation(wt[:, 4 * g:4 * g + w, :].rearrange("p j s -> p (j s)"),
                                   ptw[:, (g + s) % 2, 0:w * P], ACT.Copy).then_inc(sem("ta"), 1)
                eng.wait_ge(sem("abt"), k + 1)
                eng.activation(abT[:, :, :].rearrange("p c n -> p (c n)"), pab, ACT.Copy).then_inc(sem("abfree"), 1)
                eng.wait_ge(sem("ss"), k + 1)
                eng.activation(nrm[:, 1:2], nrm[:, 0:1], ACT.Sqrt).then_inc(sem("root"), 1)
            skewed(eng, NT, tile)

        @block.tensor
        def _(eng):
            mm = lambda o, l, r_, st, sp: eng.matmul(o, l, r_, start=st, stop=sp, skip_group_check=True)
            eng.wait_ge(sem("const"), 1)

            def edge(st, sp):
                for h in range(2):
                    for t in (pc, pd, pw):
                        last = mm(t[:, h, :], identb[:, :], zbb[:, :], st, sp)
                return last
            edge(True, False).then_inc(sem("eqfree"), 2)
            eng.wait_ge(sem("run"), 1)
            eng.transpose(pg[0:1, 0:P], st[:, 4:5], ident[:, :]).then_inc(sem("run_t"), 1)
            blocks, inner = shifts(eng)
            with eng.Fori(0, blocks) as b:
                with eng.Fori(0, inner) as i:
                    for s in range(2):
                        eng.wait_ge(sem("eq"), (b * inner + i) * 4 + 2 * s + 2)
                        for h in range(2):
                            c = slice(h * HALF, (h + 1) * HALF)
                            mm(pc[:, h, 0:HALF], identb[:, :], eqF[:, s, c], False, False)
                            mm(pd[:, h, 0:HALF], identb[:, :], eqB[:, s, c], False, False)
                            last = mm(pw[:, h, 0:HALF], ident[:, :], wF[:, s, c], False, False)
                        last.then_inc(sem("eqfree"), 1)
            edge(False, True).then_inc(sem("sums"), 1)
            eng.wait_ge(sem("edges"), 1)
            eng.wait_ge(sem("turn_in"), 96)
            for n, t in enumerate((pc, pd, pw)):
                for b in range(QB):
                    last = eng.transpose(t[:, b // 4, (b % 4) * P:(b % 4 + 1) * P], rl[:, n, b, :], ident[:, :])
            last.then_inc(sem("cols"), 1)
            eng.wait_ge(sem("gm"), 1)
            eng.transpose(pg[0:NT, 0:P], gm[:, :], ident[:, :]).then_inc(sem("gm_t"), 1)
            eng.wait_ge(sem("gmax"), 1)
            eng.matmul(pg[0:1, 256:256 + NT], gmax[:, :], ident[0:NT, 0:NT], start=True, stop=True).then_inc(sem("gmax_t"), 1)
            mm(ph, identb[:, :], zbb[:, 0:2 * NT], True, False).then_inc(sem("hfree"), 1)

            def degrees(g, s, r):
                eng.wait_ge(sem("hot"), 2 * g + 2)
                for c in range(G):
                    last = mm(ph, hlo[:, s, c, :], hhi[:, s, c, :, :].rearrange("p a n -> p (a n)"), False, False)
                last.then_inc(sem("hfree"), 1)
            skewed(eng, NG, degrees)
            mm(ph, identb[:, :], zbb[:, 0:2 * NT], False, True).then_inc(sem("deg"), 1)
            eng.wait_ge(sem("u"), 1)
            eng.wait_ge(sem("ld3"), 32)

            def tile(k, s, r):
                eng.wait_ge(sem(f"tk{s}"), 16 * r + 16)
                eng.wait_ge(sem("ab"), k + 1)
                for j in range(NT):
                    last = eng.matmul(pq[:, s, 0:D + 1], tk[:, s, j, :, 0], hx[:, j, :], start=j == 0, stop=j == NT - 1)
                last.then_inc(sem("q"), 1)
                for g in range(7):
                    for c, bank, free, ready in ((0, ptc, "tv", "tc"), (1, ptw, "ta", "tw")):
                        eng.wait_ge(sem(free), 7 * k + g + 13)
                        for j in range(4 * g, min(NT, 4 * g + 4)):
                            o = (j - 4 * g) * P
                            last = eng.transpose(bank[:, (g + s) % 2, o:o + P], tk[:, s, j, :, c], ident[:, :])
                        last.then_inc(sem(ready), 1)
                eng.wait_ge(sem("ab"), k + 3)
                for c in range(4):
                    last = eng.transpose(pab[:, c * P:(c + 1) * P], ab[:, c // 2, (c % 2) * P:(c % 2 + 1) * P], ident[:, :])
                last.then_inc(sem("abt"), 1)
                eng.wait_ge(sem("abfree"), k + 2)
                for c in range(4):
                    last = eng.matmul(pe, abT[:, c, :], wl0[:, c, :], start=c == 0, stop=c == 3)
                last.then_inc(sem("e"), 1)
            skewed(eng, NT, tile)

PARTS = [range(0, 7), range(7, 13), range(13, 19), range(19, NT)]


def phase_l1(nc, sem, sb, a):
    psum, xs, hx, ident, dinv = a.psum, a.xs, a.hx, a.ident, a.dinv
    with ExitStack() as ctx:
        def buf(name, shape, dt=F32):
            return sb(name, shape, dt, ctx)
        s_ = lambda n: sem("l1_" + n)
        wt = buf("l1wt", [P, 2, NT, P])
        w = buf("l1w", [P, 6, D])
        col = buf("l1col", [P, 4])
        b2 = buf("l1b2", [P, D])
        g1, g2 = buf("g1", [P, D]), buf("g2", [P, D])
        gT, h7T, hT = (buf(n, [P, 2, P]) for n in ("gT", "h7T", "hT"))
        res = buf("l1res", [P, D])
        pq, pA, pB, pC, pD = psum[:, 0:2, 0:D], psum[:, 2, 0:D], psum[:, 3, 0:D], psum[:, 4, 0:D], psum[:, 5, 0:D]
        block = ctx.enter_context(nc.Block())

        @block.sync
        def _(eng):
            eng.dma_start(w[:, :, :], a.w1.rearrange("(c p) o -> p c o", p=P)).then_inc(s_("par"), 16)
            eng.dma_start(col[:, :], a.cols).then_inc(s_("par"), 16)
            eng.dma_start(b2[:, :], a.vecs[1:2, :].to_broadcast([P, D])).then_inc(s_("par"), 16)

            def load(k, s, r):
                if not isinstance(k, int):
                    eng.wait_ge(s_("q"), k)
                eng.dma_start(wt[:, s, :, :], a.weights_t.ap()[bass.ds(k, 1), :, :, :].rearrange("a p k s -> (a p) k s"))\
                   .then_inc(s_(f"wt{s}"), 16)
            skewed(eng, NT, load)

        @block.tensor
        def _(eng):
            eng.sem_inc(s_("q"), 1)
            eng.wait_ge(s_("par"), 48)
            mm = eng.matmul

            def step(cur, prev):
                def part(n):
                    if cur:
                        k, s, r = cur
                        if n == 0:
                            eng.wait_ge(s_(f"wt{s}"), 16 * r + 16)
                        for t in PARTS[n]:
                            last = mm(pq[:, s, :], wt[:, s, t, :], hx[:, t, 0:D], start=t == 0, stop=t == NT - 1)
                        if n == 3:
                            last.then_inc(s_("q"), 1)
                part(0)
                if prev:
                    k = prev[0]
                    eng.wait_ge(s_("g"), k + 1)
                    for c in range(2):
                        last = eng.transpose(pA[:, c * P:(c + 1) * P], g2[:, c * P:(c + 1) * P], ident[:, :])
                    last.then_inc(s_("A"), 1)
                part(1)

                def dense(ready, w0, rhs, ps, done):
                    if prev:
                        eng.wait_ge(s_(ready), k + 1)
                        for m in range(2):
                            for c in range(2):
                                last = mm(ps[:, m * P:(m + 1) * P], w[:, w0 + c, m * P:(m + 1) * P], rhs[:, c, :],
                                          start=c == 0, stop=c == 1)
                        last.then_inc(s_(done), 1)
                dense("gT", 0, gT, pB, "B")
                part(2)
                dense("h7T", 2, h7T, pC, "C")
                part(3)
                if prev:
                    eng.wait_ge(s_("hT"), k + 1)
                    eng.wait_ge(s_("x"), k + 1)
                    for c in range(2):
                        last = mm(pD, hT[:, c, :], w[:, 4 + c, :], start=c == 0, stop=c == 1)
                    last.then_inc(s_("D"), 1)
            overlapped(eng, NT, step)

        @block.scalar
        def _(eng):
            def tile(k, s, r):
                eng.wait_ge(s_("A"), k + 1)
                eng.activation(gT[:, :, :].rearrange("p c n -> p (c n)"), pA, ACT.Copy).then_inc(s_("gT"), 1)
                eng.wait_ge(s_("B"), k + 1)
                eng.activation(h7T[:, 0, :], pB[:, 0:P], ACT.Identity, bias=col[:, 0:1])
                eng.activation(h7T[:, 1, :], pB[:, P:D], ACT.Identity, bias=col[:, 1:2]).then_inc(s_("h7T"), 1)
                eng.wait_ge(s_("C"), k + 1)
                eng.activation(hT[:, 0, :], pC[:, 0:P], ACT.Relu, bias=col[:, 2:3])
                eng.activation(hT[:, 1, :], pC[:, P:D], ACT.Relu, bias=col[:, 3:4]).then_inc(s_("hT"), 1)
            eng.wait_ge(s_("par"), 48)
            skewed(eng, NT, tile)

        @block.vector
        def _(eng):
            ch, ch2 = Chain(eng, s_("dve")), Chain(eng, s_("dve2"))
            eng.wait_ge(s_("par"), 48)
            eng.sem_inc(s_("x"), 1)

            def main(k, s, r):
                eng.wait_ge(s_("q"), k + 2)
                eng.tensor_tensor(g1[:, :], pq[:, s, :], hx[:, bass.ds(k, 1), 0:D].rearrange("p a d -> p (a d)"), ALU.add).then_inc(s_("g1"), 1)
                eng.wait_ge(s_("g1"), k + 1)
                eng.tensor_scalar(g2[:, :], g1[:, :], dinv[:, bass.ds(k, 1)], None, ALU.mult).then_inc(s_("g"), 1)

            def late3(k, s, r):
                ch.n, ch.rounds = 0, 2 * k
                eng.wait_ge(s_("D"), k + 1)
                xk = xs[:, bass.ds(k, 1), :].rearrange("p a d -> p (a d)")
                eng.tensor_tensor(res[:, :], pD, b2[:, :], ALU.add).then_inc(s_("x"), 1)
                eng.wait_ge(s_("x"), k + 2)
                ch.do(eng.tensor_tensor(xk, xk, res[:, :], ALU.add))
                ch.after()
                a.tile_stats(ch, k)
                assert ch.n == 2
            skewed(eng, NT, main, late3)


def phase_l2(nc, sem, sb, a):
    psum, xs, hx, ident = a.psum, a.xs, a.hx, a.ident
    with ExitStack() as ctx:
        def buf(name, shape, dt=F32):
            return sb(name, shape, dt, ctx)
        s_ = lambda n: sem("l2_" + n)
        ca, cb = buf("ca", [P, 2, NT, P]), buf("cb", [P, 2, NT, P])
        ys = buf("ys", [P, NT, D])
        w = buf("l2w", [P, 4, D])
        bc = buf("l2bc", [P, 4, D])
        q = buf("l2q", [P, D + 1])
        aT = buf("l2aT", [P, 4, P])
        y1 = buf("y1", [P, D])
        rsk = buf("rsk", [P, 2])
        sq = buf("l2sq", [P, 2, D])
        ones = buf("ones", [P, 2, P])
        mean, var, sd, A = (buf(n, [P, D]) for n in ("l2mean", "l2var", "l2sd", "l2A"))
        pq, pA, pY, pM, pV = psum[:, 0:2, 0:D + 1], psum[:, 2, :], psum[:, 3, 0:D], psum[:, 4, 0:D], psum[:, 5, 0:D]
        REAL = N - (NT - 1) * P
        block = ctx.enter_context(nc.Block())

        @block.sync
        def _(eng):
            eng.dma_start(w[:, :, :], a.w2.rearrange("(c p) o -> p c o", p=P)).then_inc(s_("par"), 16)
            for n in range(4):
                eng.dma_start(bc[:, n, :], a.vecs[2 + n:3 + n, :].to_broadcast([P, D])).then_inc(s_("par"), 16)

            def load(k, s, r):
                if not isinstance(k, int):
                    eng.wait_ge(s_("q"), k)
                for t, d in ((ca, a.counts), (cb, a.counts_t)):
                    eng.dma_start(t[:, s, :, :], d.ap()[bass.ds(k, 1), :, :, :].rearrange("a p k s -> (a p) k s"))\
                       .then_inc(s_(f"c{s}"), 16)
            skewed(eng, NT, load)

        @block.gpsimd
        def _(eng):
            eng.memset(ones[:, :, :], 1.0).then_inc(s_("ones0"), 1)
            eng.wait_ge(s_("ones0"), 1)
            eng.affine_select(out=ones[:, 1, :], in_=ones[:, 1, :], compare_op=ALU.is_gt, fill=0.0,
                              base=REAL, pattern=[[0, P]], channel_multiplier=-1).then_inc(s_("ones"), 1)

        @block.tensor
        def _(eng):
            eng.sem_inc(s_("q"), 1)
            eng.wait_ge(s_("par"), 80)
            mm = eng.matmul

            def step(cur, prev):
                def part(n):
                    if cur:
                        k, s, r = cur
                        if n == 0:
                            eng.wait_ge(s_("sum"), k + 1)
                        for t in PARTS[n]:
                            last = mm(pq[:, s, :], ca[:, s, t, :], hx[:, t, :], start=t == 0, stop=t == NT - 1)
                        if n == 3:
                            last.then_inc(s_("q"), 1)
                part(0)
                part(1)
                if prev:
                    k = prev[0]
                    eng.wait_ge(s_("g"), k + 1)
                    for c in range(2):
                        last = eng.transpose(pA[:, c * P:(c + 1) * P], y1[:, c * P:(c + 1) * P], ident[:, :])
                    for c in range(2):
                        last = eng.transpose(pA[:, (2 + c) * P:(3 + c) * P], q[:, c * P:(c + 1) * P], ident[:, :])
                    last.then_inc(s_("A"), 1)
                part(2)
                part(3)
                if prev:
                    eng.wait_ge(s_("aT"), k + 1)
                    eng.wait_ge(s_("y"), k + 1)
                    for c in range(4):
                        last = mm(pY, aT[:, c, :], w[:, c, :], start=c == 0, stop=c == 3)
                    last.then_inc(s_("Y"), 1)
            overlapped(eng, NT, step)
            eng.wait_ge(s_("ones"), 1)
            eng.wait_ge(s_("y"), NT + 1)
            for t in range(NT):
                last = mm(pM, ones[:, t // (NT - 1), :], ys[:, t, :], start=t == 0, stop=t == NT - 1)
            last.then_inc(s_("mean"), 1)

            def square(k, s, r):
                eng.wait_ge(s_("sq"), k + 1)
                o = 1 if isinstance(k, int) and k == NT - 1 else 0
                mm(pV, ones[:, o, :], sq[:, s, :], start=isinstance(k, int) and k == 0, stop=o == 1,
                   skip_group_check=True).then_inc(s_("sqfree"), 1)
            square(0, 0, 0)
            with eng.Fori(0, NT // 2 - 1) as i:
                square(2 * i + 1, 1, i)
                square(2 * i + 2, 0, i)
            square(NT - 2, 1, 0)
            square(NT - 1, 0, 0)

        @block.scalar
        def _(eng):
            def tile(k, s, r):
                eng.wait_ge(s_("A"), k + 1)
                eng.activation(aT[:, :, :].rearrange("p c n -> p (c n)"), pA, ACT.Copy).then_inc(s_("aT"), 1)
            skewed(eng, NT, tile)
            eng.wait_ge(s_("cent"), 1)
            eng.sem_inc(s_("sqfree"), 2)

            def square(k, s, r):
                eng.wait_ge(s_("sqfree"), k + 1)
                eng.activation(sq[:, s, :], ys[:, bass.ds(k, 1), :].rearrange("p a d -> p (a d)"), ACT.Square).then_inc(s_("sq"), 1)
            skewed(eng, NT, square)
            eng.wait_ge(s_("var"), 1)
            eng.activation(sd[:, :], var[:, :], ACT.Sqrt, bias=a.eps[:, :]).then_inc(s_("sd"), 1)

        @block.vector
        def _(eng):
            eng.wait_ge(s_("par"), 80)
            eng.sem_inc(s_("y"), 1)

            def add(k, s, r):
                eng.wait_ge(s_(f"c{s}"), 32 * r + 32)
                eng.tensor_tensor(ca[:, s, :, :], ca[:, s, :, :], cb[:, s, :, :], ALU.add).then_inc(s_("sum"), 1)

            def take(k, s, r):
                eng.wait_ge(s_("q"), k + 2)
                eng.tensor_copy(y1[:, :], hx[:, bass.ds(k, 1), 0:D].rearrange("p a d -> p (a d)"))
                eng.tensor_copy(q[:, :], pq[:, s, :]).then_inc(s_("g"), 1)

            def late(k, s, r):
                eng.wait_ge(s_("Y"), k + 1)
                yk = ys[:, bass.ds(k, 1), :].rearrange("p a d -> p (a d)")
                eng.tensor_tensor(yk, pY, bc[:, 0, :], ALU.add).then_inc(s_("y0"), 1)
                eng.wait_ge(s_("y0"), k + 1)
                eng.scalar_tensor_tensor(out=yk, in0=bc[:, 1, :], scalar=rsk[:, s:s + 1], in1=yk,
                                         op0=ALU.mult, op1=ALU.add).then_inc(s_("y"), 1)

            def take2(k, s, r):
                take(k, s, r)
                if not (isinstance(k, int) and k == 0):
                    eng.wait_ge(s_("y"), k)
                eng.tensor_copy(rsk[:, s:s + 1], pq[:, s, D:D + 1]).then_inc(s_("rs"), 1)

            def late2(k, s, r):
                eng.wait_ge(s_("rs"), k + 1)
                late(k, s, r)
            add(0, 0, 0)
            add(1, 1, 0)
            take2(0, 0, 0)
            with eng.Fori(0, NT // 2 - 1) as i:
                add(2 * i + 2, 0, i + 1)
                take2(2 * i + 1, 1, i)
                late2(2 * i, 0, i)
                add(2 * i + 3, 1, i + 1)
                take2(2 * i + 2, 0, i + 1)
                late2(2 * i + 1, 1, i)
            add(NT - 1, 0, NT // 2)
            take2(NT - 2, 1, NT // 2 - 1)
            late2(NT - 3, 0, NT // 2 - 1)
            take2(NT - 1, 0, NT // 2)
            late2(NT - 2, 1, NT // 2 - 1)
            late2(NT - 1, 0, NT // 2)
            ch = Chain(eng, s_("dve"))
            do, after = ch.do, ch.after
            wide = lambda t: t[:, :].unsqueeze(1).to_broadcast([P, NT, D])
            eng.wait_ge(s_("mean"), 1)
            do(eng.tensor_scalar(mean[:, :], pM, 1.0 / N, None, ALU.mult))
            after()
            do(eng.tensor_tensor(ys[:, :, :], ys[:, :, :], wide(mean), ALU.subtract))
            after()
            eng.sem_inc(s_("cent"), 1)
            eng.wait_ge(s_("sqfree"), NT + 2)
            do(eng.tensor_scalar(var[:, :], pV, 1.0 / N, None, ALU.mult))
            after()
            eng.sem_inc(s_("var"), 1)
            eng.wait_ge(s_("sd"), 1)
            do(eng.reciprocal(A[:, :], sd[:, :]))
            after()
            do(eng.tensor_tensor(A[:, :], A[:, :], bc[:, 2, :], ALU.mult))
            after()
            do(eng.tensor_tensor(ys[:, :, :], ys[:, :, :], wide(A), ALU.mult))
            after()
            do(eng.tensor_tensor(ys[:, :, :], ys[:, :, :], bc[:, 3:4, :].to_broadcast([P, NT, D]), ALU.add))
            after()
            do(eng.scalar_tensor_tensor(out=xs[:, :, :], in0=ys[:, :, :], scalar=0.0, in1=xs[:, :, :], op0=ALU.max, op1=ALU.add))
            after()
            a.layernorm_stats(ch)


BIG = 3.0e38
H = 4
HD = D // H
FW = HD + 1
PB = 7


def ring4(eng, step):
    assert NT % 4 == 1
    step((0, 0, 0), None)
    with eng.Fori(0, NT // 4) as i:
        for u in range(1, 5):
            step((4 * i + u, u % 4, 2 * i + u // 2), (4 * i + u - 1, u - 1, 2 * i + (u - 1) // 2))
    step(None, (NT - 1, 0, NT // 2))


def heads(eng, body):
    with eng.Fori(0, H // 2) as i:
        for u in range(2):
            body(2 * i + u, u, i)


def phase_l3(nc, sem, sb, a):
    psum, xs, hx, ident = a.psum, a.xs, a.hx, a.ident
    rows = nc.dram_tensor("rows", [2 * H, NP], F32)
    rrows = nc.dram_tensor("rrows", [2 * H, NP], F32)
    s_ = lambda n: sem("l3_" + n)
    flat2 = lambda t: t.rearrange("p a d -> p (a d)")
    with ExitStack() as outer:
        ftx = sb("ftx", [P, NT, H, FW], F32, outer)
        sc = sb("sc", [P, NT, 2 * H], F32, outer)
        sc02 = sb("sc02", [P, NT, 2 * H], F32, outer)
        rr = sb("rr", [P, NT, 2 * H], F32, outer)

        def to_rows(eng, src, dst_ps, ready, took):
            for g in range(7):
                eng.wait_ge(s_(took), g + 1)
                for t in range(4 * g, min(NT, 4 * g + 4)):
                    last = eng.transpose(dst_ps[0:2 * H, g % 2, (t - 4 * g) * P:(t - 4 * g + 1) * P], src[:, t, :], ident[:, :])
                last.then_inc(s_(ready), 1)

        def take_rows(eng, dst_sb, src_ps, ready, took):
            eng.sem_inc(s_(took), 2)
            for g in range(7):
                w = min(4, NT - 4 * g) * P
                eng.wait_ge(s_(ready), g + 1)
                eng.tensor_copy(dst_sb[:, 4 * g * P:4 * g * P + w], src_ps[0:2 * H, g % 2, 0:w]).then_inc(s_(took), 1)

        with ExitStack() as ctx:
            def buf(name, shape, dt=F32):
                return sb(name, shape, dt, ctx)
            w = buf("l3w", [P, 2, D + 2 * H])
            at = buf("l3at", [P, 2, D])
            prod = buf("l3prod", [P, 2, D])
            hT = buf("l3hT", [P, 2, 2, P])
            rsb = buf("rsb", [2 * H, NP])
            pT, pF = psum[:, 0:2, 0:D], psum[:, 2:4, 0:D + 2 * H]
            pR = psum[:, 4:6, :]
            block = ctx.enter_context(nc.Block())

            @block.sync
            def _(eng):
                eng.dma_start(w[:, :, 0:D], a.w3.rearrange("(c p) o -> p c o", p=P)).then_inc(s_("par"), 16)
                for n in range(2):
                    eng.dma_start(at[:, n, :], a.vecs[6 + n:7 + n, :].to_broadcast([P, D])).then_inc(s_("par"), 16)
                eng.wait_ge(s_("rtook"), 2 + 7)
                eng.dma_start(rows.ap(), rsb[:, :]).then_inc(s_("rows"), 16)
                eng.wait_ge(s_("rows"), 16)

            @block.vector
            def _(eng):
                ch = Chain(eng, s_("dve"))
                eng.wait_ge(s_("par"), 48)
                for n in range(2):
                    ch.do(eng.tensor_tensor(prod[:, :, :], w[:, :, 0:D], at[:, n:n + 1, :].to_broadcast([P, 2, D]), ALU.mult))
                    ch.after()
                    ch.do(eng.tensor_reduce(w[:, :, D + H * n:D + H * n + H],
                                            prod[:, :, :].rearrange("p c (h d) -> p c h d", h=H), AX.X, ALU.add))
                    ch.after()
                ch.do(eng.memset(ftx[:, :, :, HD:FW], 1.0))
                ch.after()
                eng.sem_inc(s_("w"), 1)

                eng.wait_ge(s_("sc"), NT)
                eng.tensor_scalar(sc02[:, :, :], sc[:, :, :], 0.2, None, ALU.mult)
                take_rows(eng, rsb, pR, "rready", "rtook")

            @block.scalar
            def _(eng):
                def evac(k, s, r):
                    eng.wait_ge(s_("T"), k + 1)
                    eng.activation(flat2(hT[:, s, :, :]), pT[:, s, :], ACT.Copy).then_inc(s_("hT"), 1)

                def feats(k, s, r):
                    eng.wait_ge(s_("F"), k + 1)
                    eng.activation(ftx[:, bass.ds(k, 1), :, 0:HD].rearrange("p a h d -> p (a h) d"),
                                   pF[:, s, 0:D].rearrange("p (h d) -> p h d", h=H), ACT.Copy).then_inc(s_("ft"), 1)
                    eng.activation(flat2(sc[:, bass.ds(k, 1), :]), pF[:, s, D:D + 2 * H], ACT.Copy).then_inc(s_("sc"), 1)
                eng.sem_inc(s_("ft"), 2)
                eng.wait_ge(s_("w"), 1)
                skewed(eng, NT, evac, feats)

            def product(eng, k):
                s = k % 2
                eng.wait_ge(s_("hT"), k + 1)
                eng.wait_ge(s_("ft"), k + 1)
                if k > 1:
                    eng.wait_ge(s_("sc"), k - 1)
                for c in range(2):
                    last = eng.matmul(pF[:, s, :], hT[:, s, c, :], w[:, c, :], start=c == 0, stop=c == 1)
                last.then_inc(s_("F"), 1)

            @block.tensor
            def _(eng):
                eng.wait_ge(s_("w"), 1)

                for k in range(NT):
                    s = k % 2
                    for c in range(2):
                        last = eng.transpose(pT[:, s, c * P:(c + 1) * P], hx[:, k, c * P:(c + 1) * P], ident[:, :])
                    last.then_inc(s_("T"), 1)
                    if k:
                        product(eng, k - 1)
                product(eng, NT - 1)
                eng.wait_ge(s_("sc"), NT)
                to_rows(eng, sc, pR, "rready", "rtook")


        with ExitStack() as ctx:
            def buf(name, shape, dt=F32):
                return sb(name, shape, dt, ctx)
            a1 = buf("a1", [P, H, NP])
            cm = buf("cm", [P, 2, NT, P])
            mb = buf("mb", [P, 2, NP])
            junk = buf("junk", [P, NP], BF16)
            mx = buf("mx", [P, 2, H])
            top = buf("top", [P, NT, H])
            x1, x2, some = buf("x1", [P, NT, H]), buf("x2", [P, NT, H]), buf("some", [P, NT, H])
            rsb = buf("rsb2", [2 * H, NP])
            pR = psum[:, 4:6, :]
            block = ctx.enter_context(nc.Block())

            @block.sync
            def _(eng):
                for h in range(H):
                    eng.dma_start(a1[:, h, :], rows.ap()[h:h + 1, :].to_broadcast([P, NP])).then_inc(s_("a1"), 16)

                def load(k, s, r):
                    if not isinstance(k, int):
                        eng.wait_ge(s_("mb"), k)
                    eng.dma_start(cm[:, s, :, :], a.counts_t.ap()[:, :, bass.ds(k, 1), :].rearrange("j p k s -> p (j k) s"))\
                       .then_inc(s_(f"cm{s}"), 16)
                skewed(eng, NT, load)
                eng.wait_ge(s_("r2took"), 2 + 7)
                eng.dma_start(rrows.ap(), rsb[:, :]).then_inc(s_("rrows"), 16)
                eng.wait_ge(s_("rrows"), 16)

            @block.gpsimd
            def _(eng):
                eng.sem_inc(s_("mb"), 1)

                def mask(k, s, r):
                    eng.wait_ge(s_(f"cm{s}"), 16 * r + 16)
                    eng.wait_ge(s_("top"), k + 1)
                    eng.sem_inc(s_("pass_p"), 1)
                    eng.tensor_scalar(mb[:, s, :], cm[:, s, :, :].rearrange("p j s -> p (j s)"), 0.0, -BIG,
                                      ALU.is_equal, ALU.mult).then_inc(s_("mb"), 1)
                skewed(eng, NT, mask)

            @block.vector
            def _(eng):
                eng.sem_inc(s_("top"), 2)
                eng.wait_ge(s_("a1"), 64)

                def reduce(k, s, r):
                    eng.wait_ge(s_("mb"), k + 2)
                    if not isinstance(k, int):
                        eng.wait_ge(s_("top"), k + 1)
                    eng.sem_inc(s_("pass_v"), 1)
                    for h in range(H):
                        eng.tensor_tensor_reduce(out=junk[:, :], in0=mb[:, s, :], in1=a1[:, h, :], scale=1.0, scalar=-BIG,
                                                 op0=ALU.add, op1=ALU.max, accum_out=mx[:, s, h:h + 1]).then_inc(s_("head"), 1)
                        eng.wait_ge(s_("head"), H * k + h + 1)
                        eng.sem_inc(s_("pass_v"), 1)
                    eng.tensor_copy(flat2(top[:, bass.ds(k, 1), :]), mx[:, s, :]).then_inc(s_("top"), 1)
                skewed(eng, NT, reduce)
                eng.wait_ge(s_("top"), NT + 2)
                ch = Chain(eng, s_("dve2"))
                do, after = ch.do, ch.after
                a2, a02 = sc[:, :, H:2 * H], sc02[:, :, H:2 * H]
                do(eng.tensor_tensor(x1[:, :, :], top[:, :, :], a2, ALU.add))
                do(eng.tensor_scalar(some[:, :, :], top[:, :, :], -0.5 * BIG, None, ALU.is_gt))
                after()
                do(eng.tensor_scalar(x2[:, :, :], x1[:, :, :], 0.2, None, ALU.mult))
                after()
                do(eng.tensor_tensor(x1[:, :, :], x1[:, :, :], x2[:, :, :], ALU.max))
                after()
                do(eng.tensor_tensor(x1[:, :, :], x1[:, :, :], some[:, :, :], ALU.mult))
                after()
                do(eng.tensor_tensor(rr[:, :, 0:H], a2, x1[:, :, :], ALU.subtract))
                do(eng.tensor_tensor(rr[:, :, H:2 * H], a02, x1[:, :, :], ALU.subtract))
                after()
                eng.sem_inc(s_("rr"), 1)
                take_rows(eng, rsb, pR, "r2ready", "r2took")

            @block.tensor
            def _(eng):
                eng.wait_ge(s_("rr"), 1)
                to_rows(eng, rr, pR, "r2ready", "r2took")

        with ExitStack() as ctx:
            def buf(name, shape, dt=F32):
                return sb(name, shape, dt, ctx)
            rb = buf("rb", [P, 2, 2, NP])
            t4 = buf("t4", [P, 4, NP])
            cj = buf("cj", [P, 2, NT, P])
            den = buf("den", [P, NT])
            rden = buf("rden", [P, NT])
            o = hx[:, :, 0:D]
            block = ctx.enter_context(nc.Block())
            acc = [psum[:, 4 * u:4 * u + 4, :] for u in range(2)]

            def tail(c):
                return t4[:, :, :].rearrange("p s n -> p (s n)")[:, 5 * c * D:5 * (c + 1) * D].rearrange("p (t d) -> p t d", d=D)

            def at_(u, k):
                return acc[u][:, k // PB, (k % PB) * FW:(k % PB + 1) * FW]

            @block.sync
            def _(eng):
                def head(h, u, i):
                    eng.wait_ge(s_("ev"), h + 1)
                    for n in range(2):
                        eng.dma_start(rb[:, u, n, :], rrows.ap()[bass.ds(H * n + h, 1), :].to_broadcast([P, NP]))\
                           .then_inc(s_(f"rb{u}"), 16)

                    def load(cur, prev):
                        if cur:
                            k, s, half = cur
                            eng.wait_ge(s_("pm"), NT * h + k + (2 if isinstance(k, int) else 1))
                            eng.dma_start(cj[:, s % 2, :, :], a.counts.ap()[:, :, bass.ds(k, 1), :].rearrange("k p j d -> p (k j) d"))\
                               .then_inc(s_(f"cj{s % 2}"), 16)
                    ring4(eng, load)
                heads(eng, head)

            @block.scalar
            def _(eng):
                def head(h, u, i):
                    def step(cur, prev):
                        if cur:
                            k, s, half = cur
                            eng.wait_ge(s_(f"rb{u}"), 32 * i + 32)
                            eng.wait_ge(s_("mm"), NT * h + k + (4 if isinstance(k, int) else 1))
                            eng.activation(t4[:, s, :], rb[:, u, 0, :], ACT.Identity,
                                           bias=flat2(sc[:, bass.ds(k, 1), bass.ds(h, 1)])).then_inc(s_("t1"), 1)
                        if prev:
                            k, s, half = prev
                            eng.wait_ge(s_("mx"), NT * h + k + 1)
                            eng.activation(t4[:, s, :], t4[:, s, :], ACT.Exp).then_inc(s_("ex"), 1)
                    ring4(eng, step)
                heads(eng, head)
                for c in range(5):
                    eng.wait_ge(s_("neg"), c + 1)
                    t = tail(c)
                    eng.activation(t, t, ACT.Exp).then_inc(s_("elu"), 1)


            @block.vector
            def _(eng):
                eng.sem_inc(s_("ev"), 2)
                eng.sem_inc(s_("pm"), 2)

                def head(h, u, i):
                    def step(cur, prev):
                        if cur:
                            k, s, half = cur
                            eng.wait_ge(s_("t1"), NT * h + k + 1)
                            eng.scalar_tensor_tensor(out=t4[:, s, :], in0=rb[:, u, 1, :],
                                                     scalar=flat2(sc02[:, bass.ds(k, 1), bass.ds(h, 1)]),
                                                     in1=t4[:, s, :], op0=ALU.add, op1=ALU.max).then_inc(s_("mx"), 1)
                        if prev:
                            k, s, half = prev
                            eng.wait_ge(s_("ex"), NT * h + k + 1)
                            loads = (NT - NT // 2, NT // 2)[s % 2]
                            eng.wait_ge(s_(f"cj{s % 2}"), 16 * (loads * h + half + 1))
                            eng.scalar_tensor_tensor(out=t4[:, s, :], in0=t4[:, s, :], scalar=1.0,
                                                     in1=cj[:, s % 2, :, :].rearrange("p k d -> p (k d)"),
                                                     op0=ALU.min, op1=ALU.mult).then_inc(s_("pm"), 1)
                    ring4(eng, step)
                    eng.wait_ge(s_("mm"), NT * h + NT + 4)
                    for b in range(4):
                        n = min(PB, NT - PB * b)
                        av = acc[u][:, b, 0:n * FW].rearrange("p (t f) -> p t f", f=FW)
                        eng.tensor_scalar(den[:, PB * b:PB * b + n], av[:, :, HD], 1e-30, None, ALU.max).then_inc(s_("dn"), 1)
                    eng.wait_ge(s_("dn"), 5 * h + 4)
                    eng.reciprocal(rden[:, :], den[:, :]).then_inc(s_("dn"), 1)
                    eng.wait_ge(s_("dn"), 5 * h + 5)
                    for b in range(4):
                        n = min(PB, NT - PB * b)
                        av = acc[u][:, b, 0:n * FW].rearrange("p (t f) -> p t f", f=FW)
                        last = eng.tensor_tensor(o[:, PB * b:PB * b + n, bass.ds(HD * h, HD)], av[:, :, 0:HD],
                                                 rden[:, PB * b:PB * b + n].unsqueeze(2).to_broadcast([P, n, HD]), ALU.mult)
                        last.then_inc(s_("ev"), 1) if b == 3 else last.then_inc(s_("evs"), 1)
                    eng.wait_ge(s_("evs"), 3 * h + 3)
                heads(eng, head)
                eng.wait_ge(s_("ev"), H + 2)
                for c in range(5):
                    oc, xc = o[:, 5 * c:5 * c + 5, :], xs[:, 5 * c:5 * c + 5, :]
                    eng.tensor_scalar(tail(c), oc, 0.0, None, ALU.min).then_inc(s_("neg"), 1)
                    eng.scalar_tensor_tensor(out=xc, in0=oc, scalar=0.0, in1=xc, op0=ALU.max, op1=ALU.add).then_inc(s_("pos"), 1)
                for c in range(5):
                    xc = xs[:, 5 * c:5 * c + 5, :]
                    eng.wait_ge(s_("elu"), c + 1)
                    eng.wait_ge(s_("pos"), c + 1)
                    eng.scalar_tensor_tensor(out=xc, in0=tail(c), scalar=-1.0, in1=xc, op0=ALU.add, op1=ALU.add)

            @block.tensor
            def _(eng):
                eng.sem_inc(s_("mm"), 4)

                def head(h, u, i):
                    def step(cur, prev):
                        if cur:
                            k, s, half = cur
                            if isinstance(k, int):
                                eng.wait_ge(s_("ev"), h + 1)
                            eng.wait_ge(s_("pm"), NT * h + k + 3)
                            for d in range(NT):
                                last = eng.matmul(at_(u, d), t4[:, s, d * P:(d + 1) * P],
                                                  ftx[:, bass.ds(k, 1), bass.ds(h, 1), :].rearrange("p a h d -> p (a h d)"),
                                                  start=isinstance(k, int) and d % PB == 0, stop=True, skip_group_check=True)
                            last.then_inc(s_("mm"), 1)
                    ring4(eng, step)
                heads(eng, head)


def kernel(**inp):
    import numpy as np
    import concourse.bacc as bacc
    from concourse.bass_utils import run_bass_kernel_spmd as run
    nc = bacc.Bacc("TRN2", target_bir_lowering=False, num_devices=1)
    g = {k: np.asarray(v) for k, v in inp.items()}
    a = {}
    a["x"] = g["x"]
    a["src"] = np.concatenate([g["src"], np.full(EP - E, NP - 1, np.int32)])
    a["dst"] = np.concatenate([g["dst"], np.full(EP - E, NP - 1, np.int32), NP + np.arange(EC, dtype=np.int32)])
    a["ew"] = np.concatenate([g["edge_weight"], np.zeros(EP - E, np.float32)])
    a["iota"] = np.tile(np.arange(P, dtype=np.float32), (P, 1))
    a["group"] = (np.arange(EP) // (P * GS) + 1).astype(np.float32).reshape(P, EC)
    a["vecs"] = np.stack([g["L0_gnn_b"], g["L1_gnn_b2"], g["L2_gnn_b0"], g["L2_gnn_b1"], g["L2_gnn_gamma"],
                          g["L2_gnn_beta"], g["L3_gnn_attn_l"].reshape(D), g["L3_gnn_attn_r"].reshape(D)])
    a["cols"] = np.stack([g["L1_gnn_b"].reshape(2, P), g["L1_gnn_b1"].reshape(2, P)]).reshape(4, P).T.copy()
    a["w0"] = np.concatenate([g["L0_gnn_W1"], g["L0_gnn_W2"]])
    a["w1"] = np.concatenate([g["L1_gnn_W"], g["L1_gnn_W1"], g["L1_gnn_W2"]])
    a["w2"] = np.concatenate([g["L2_gnn_W0"].T, g["L2_gnn_W1"].T])
    a["w3"] = np.ascontiguousarray(g["L3_gnn_W"].T)
    args = [nc.dram_tensor("in_" + k, v.shape, mybir.dt.from_np(v.dtype), kind="ExternalInput").ap() for k, v in a.items()]
    out = nc.dram_tensor("out_0", (N, D), F32, kind="ExternalOutput").ap()
    build(nc, *args, out)
    r = run(nc, [{"in_" + k: v for k, v in a.items()}], core_ids=[0])
    return r.results[0]["out_0"]
```

```python
import concourse.bass as bass
from concourse import mybir
from contextlib import ExitStack

F32 = mybir.dt.float32
I32 = mybir.dt.int32
BF16 = mybir.dt.bfloat16
ALU = mybir.AluOpType
ACT = mybir.ActivationFunctionType
AX = mybir.AxisListType

P = 128
N = 3125
D = 256
NT = -(-N // P)
NP = NT * P
E = 103125
EC = -(-E // P)
EP = EC * P
HALF = EC // 2
SH = 64
W = EC + SH - 1
G = 13
NG = EC // G
GS = 26
NGS = EC // GS
assert NG * G == EC and NGS * GS == EC and 2 * HALF == EC
CELLS = NP * NP
KF = EP + EC
QB = -(-EC // P)
OUT_OF_TABLE = float(2 ** 24)
LN_EPS = 1e-5


def skewed(eng, n, main, late=None):
    late = late or (lambda k, s, r: None)
    main(0, 0, 0)
    with eng.Fori(0, (n - 1) // 2) as i:
        main(2 * i + 1, 1, i)
        late(2 * i, 0, i)
        main(2 * i + 2, 0, i + 1)
        late(2 * i + 1, 1, i)
    if n % 2 == 0:
        main(n - 1, 1, n // 2 - 1)
        late(n - 2, 0, n // 2 - 1)
        late(n - 1, 1, n // 2 - 1)
    else:
        late(n - 1, 0, n // 2)


def overlapped(eng, n, step):
    assert n % 2
    step((0, 0, 0), None)
    with eng.Fori(0, (n - 1) // 2) as i:
        step((2 * i + 1, 1, i), (2 * i, 0, i))
        step((2 * i + 2, 0, i + 1), (2 * i + 1, 1, i))
    step(None, (n - 1, 0, n // 2))


class Chain:

    def __init__(self, eng, sem):
        self.eng, self.sem, self.n, self.rounds = eng, sem, 0, 0

    def do(self, ins):
        self.n += 1
        ins.then_inc(self.sem, 1)

    def after(self):
        self.eng.wait_ge(self.sem, self.rounds + self.n)

    def run(self, n, per, tile):
        start = self.n

        def counted(k, s, r):
            self.n, self.rounds = start, k * per
            tile(k, s, r)
            assert self.n - start == per, self.n - start
        skewed(self.eng, n, counted)
        self.n, self.rounds = start + n * per, 0


class Shared:
    pass


def build(nc, x_in, src, dst, ew, iota, group, vecs, cols, w0, w1, w2, w3, out):
    ctx = ExitStack()
    sems = {}

    def sem(name):
        if name not in sems:
            sems[name] = ctx.enter_context(nc.semaphore(name))
        return sems[name]

    with ctx:
        def sb(name, shape, dt=F32, c=ctx):
            return c.enter_context(nc.sbuf_tensor(name, shape, dt))

        table = nc.dram_tensor("table", [CELLS, 2], F32)
        keyflat = nc.dram_tensor("keyflat", [KF + EP + KF], F32)
        ewflat = nc.dram_tensor("ewflat", [EP + KF], F32)
        turn = nc.dram_tensor("turn", [3, QB * P * P], F32)
        counts = nc.dram_tensor("counts", [NT, P, NT, P], F32)
        counts_t = nc.dram_tensor("counts_t", [NT, P, NT, P], F32)
        weights_t = nc.dram_tensor("weights_t", [NT, P, NT, P], F32)

        psum = ctx.enter_context(nc.psum_tensor("psum", [P, 8, 512], F32))
        xs = sb("xs", [P, NT, D])
        hx = sb("hx", [P, NT, D + 1])
        ident = sb("ident", [P, P])
        rso = sb("rso", [P, NT])
        dinv = sb("dinv", [P, NT])
        stats = sb("stats", [P, NT, 6])
        mv = sb("mv", [P, NT, 2])
        rstd = sb("rstd", [P, NT])
        shift = sb("shift", [P, NT])
        eps = sb("eps", [P, 1])

        def layernorm_stats(ch):
            eng = ch.eng
            for t in range(NT):
                ch.do(eng.bn_stats(stats[:, t, :], xs[:, t, :]))
            ch.after()

        def aggregate_stats(ch):
            for t in range(NT):
                ch.do(ch.eng.bn_aggr(mv[:, t, :], stats[:, t, :]))
            ch.after()

        def tile_stats(ch, k):
            one = lambda t: t[:, bass.ds(k, 1), :].rearrange("p a d -> p (a d)")
            ch.do(ch.eng.bn_stats(one(stats), one(xs)))

        def normalize(blk, scale=None):
            with ExitStack() as c:
                sd = sb(blk + "_sd", [P, NT], F32, c)
                rs, sh = sb(blk + "_rs", [P, NT], F32, c), sb(blk + "_sh", [P, NT], F32, c)
                block = c.enter_context(nc.Block())
                t = blk + "_ln_"

                @block.scalar
                def _(eng):
                    eng.wait_ge(sem(t + "mv"), 1)
                    eng.activation(sd[:, :], mv[:, :, 1], ACT.Sqrt, bias=eps[:, :]).then_inc(sem(t + "sd"), 1)
                    eng.wait_ge(sem(t + "shift"), 1)
                    for i in range(NT):
                        eng.activation(hx[:, i, 0:D], xs[:, i, :], ACT.Relu, bias=sh[:, i:i + 1], scale=rs[:, i:i + 1])

                @block.vector
                def _(eng):
                    ch = Chain(eng, sem(t + "dve"))
                    aggregate_stats(ch)
                    eng.sem_inc(sem(t + "mv"), 1)
                    eng.wait_ge(sem(t + "sd"), 1)
                    ch.do(eng.reciprocal(rs[:, :], sd[:, :]))
                    ch.after()
                    if scale is not None:
                        ch.do(eng.tensor_tensor(rs[:, :], rs[:, :], scale[:, :], ALU.mult))
                        ch.after()
                    ch.do(eng.scalar_tensor_tensor(out=sh[:, :], in0=mv[:, :, 0], scalar=-1.0, in1=rs[:, :],
                                                   op0=ALU.mult, op1=ALU.mult))
                    ch.after()
                    eng.sem_inc(sem(t + "shift"), 1)

        shared = Shared()
        shared.x_in, shared.src, shared.dst = x_in, src, dst
        shared.ew, shared.iota, shared.group = ew, iota, group
        shared.vecs, shared.cols, shared.w0 = vecs, cols, w0
        shared.w1, shared.w2, shared.w3 = w1, w2, w3
        shared.table, shared.keyflat, shared.ewflat = table, keyflat, ewflat
        shared.turn, shared.counts, shared.counts_t = turn, counts, counts_t
        shared.weights_t, shared.psum, shared.xs = weights_t, psum, xs
        shared.hx, shared.ident, shared.rso = hx, ident, rso
        shared.dinv, shared.rstd, shared.shift = dinv, rstd, shift
        shared.mv, shared.eps, shared.layernorm_stats = mv, eps, layernorm_stats
        shared.aggregate_stats, shared.tile_stats = aggregate_stats, tile_stats
        phase_edges_and_l0(nc, sem, sb, shared)
        normalize("l1", dinv)
        phase_l1(nc, sem, sb, shared)
        normalize("l2")
        phase_l2(nc, sem, sb, shared)
        normalize("l3")
        phase_l3(nc, sem, sb, shared)
        l3_tail(nc, sem, sb, shared, out)


def phase_edges_and_l0(nc, sem, sb, a):
    psum, xs, hx, ident, rso, dinv = a.psum, a.xs, a.hx, a.ident, a.rso, a.dinv
    rstd, shift, mv, eps = a.rstd, a.shift, a.mv, a.eps
    table, keyflat, ewflat, turn = a.table.ap(), a.keyflat.ap(), a.ewflat.ap(), a.turn.ap()
    counts, counts_t, weights_t = a.counts.ap(), a.counts_t.ap(), a.weights_t.ap()
    ctx = ExitStack()
    with ctx:
        def buf(name, shape, dt=F32):
            return sb(name, shape, dt, ctx)
        tk = buf("tk", [P, 2, NT, P, 2])
        zero = tk[:, 1, :, :, :].rearrange("p j d c -> p (j d c)")
        region = buf("region", [P, 3, NP])
        cs = region[:, 0, :].rearrange("p (j d) -> p j d", j=NT)
        ct = region[:, 1, :].rearrange("p (j s) -> p j s", j=NT)
        wt = region[:, 2, :].rearrange("p (j s) -> p j s", j=NT)
        flat = region[:, :, :].rearrange("p a n -> p (a n)")

        def f(n, width=EC):
            return flat[:, n * EC:n * EC + width]
        srci, dsti, dst1, dst2, dst3, t0, t1 = (f(n).bitcast(I32) for n in range(7))
        f0, f1, key, sent = (f(n) for n in range(7, 11))
        lo, hi, cnt_e, w_e, idx_e = f(3), f(4), f(5), f(6), f(8)
        two = buf("two", [P, 5900])
        keyF, keyB, ewF = (two[:, n * W:(n + 1) * W] for n in range(3))
        eqF, eqB = (two[:, 3 * W + n * EC:3 * W + (n + 1) * EC].bitcast(BF16).rearrange("p (s c) -> p s c", s=2) for n in range(2))
        wF = two[:, 3 * W + 2 * EC:3 * W + 4 * EC].rearrange("p (s c) -> p s c", s=2)
        hlo = two[:, 0:2 * G * P].rearrange("p (s c n) -> p s c n", s=2, c=G)
        hhi = two[:, 2 * G * P:2 * G * P + 4 * G * NT].rearrange("p (s c a n) -> p s c a n", s=2, c=G, a=2)
        ewt = buf("ewt", [P, EC])
        gno = buf("gno", [P, EC])
        rl = tk[:, 0, :, :, :].rearrange("p j d c -> p (j d c)")[:, 0:3 * QB * P].rearrange("p (a q e) -> p a q e", a=3, q=QB)
        bc = buf("bc", [P, 1, D])
        idxT = buf("idxT", [P, EC], I32)
        valT = buf("valT", [P, EC, 2])
        idxs = buf("idxs", [P, 2, GS], I32)
        vals = buf("vals", [P, 2, GS, 2])
        io = buf("io", [P, P])
        identb = buf("identb", [P, P], BF16)
        zbb = buf("zbb", [P, 512], BF16)
        st = buf("st", [P, 8])
        sti = buf("sti", [P, 4], I32)
        gm = buf("gm", [P, NT])
        gmax = buf("gmax", [NT, 1])
        need = buf("need", [1, NT], I32)
        lastd, clr = buf("lastd", [1, NGS], I32), buf("clr", [1, NGS], I32)
        allclr = buf("allclr", [1, 1])
        wl0 = buf("wl0", [P, 4, D])
        hk = buf("hk", [P, D])
        q = buf("q", [P, D])
        ab = buf("ab", [P, 2, D])
        abT = buf("abT", [P, 4, P])
        e1 = buf("e1", [P, D])
        e2 = buf("e2", [P, D])
        sq = buf("sq", [P, D])
        msk = buf("msk", [P, 1])
        nrm = buf("nrm", [P, 4])
        od2 = buf("od2", [P, 2, NT])
        od3 = buf("od3", [P, 2, NT])
        pc, pd, pw = psum[:, 0:2, :], psum[:, 2:4, :], psum[:, 4:6, :]
        phr = psum[0:2 * NT, 6, 0:P]
        ph = psum[:, 7, 0:2 * NT]
        pg = psum[:, 7, :]
        pq = psum[:, 0:2, :]
        ptc, ptw = psum[:, 2:4, :], psum[:, 4:6, :]
        pab, pe = psum[:, 6, :], psum[:, 7, 0:D]

        def shifts(eng):
            eng.wait_ge(sem("shift"), 1)
            blocks = eng.value_load(sti[0:1, 1:2], min_val=1, max_val=EP // SH + 1)
            inner = eng.value_load(sti[0:1, 2:3], min_val=1, max_val=SH // 2)
            return blocks, inner

        block = ctx.enter_context(nc.Block())

        @block.sync
        def _(eng):
            rows = lambda t: t.rearrange("(p c) -> p c", p=P)
            for t, s in ((srci, a.src[0:EP]), (dsti, a.dst[0:EP]), (dst1, a.dst[1:EP + 1]),
                         (dst2, a.dst[HALF:HALF + EP]), (dst3, a.dst[HALF + 1:HALF + 1 + EP]), (ewt[:, :], a.ew)):
                eng.dma_start(t, rows(s)).then_inc(sem("ld"), 16)
            eng.dma_start(lastd[:, :], a.dst[0:EP].rearrange("(g e) -> e g", g=NGS)[EP // NGS - 1:EP // NGS, :],
                          allow_slow_non_contiguous=True)\
               .then_inc(sem("ld"), 16)
            eng.dma_start(io[:, :], a.iota).then_inc(sem("ld2"), 16)
            eng.dma_start(gno[:, :], a.group).then_inc(sem("ld2"), 16)
            eng.dma_start(xs[:, 0:NT - 1, :], a.x_in[0:(NT - 1) * P, :].rearrange("(t p) d -> p t d", p=P)).then_inc(sem("ldx"), 16)
            eng.wait_ge(sem("xpad"), 1)
            eng.dma_start(xs[0:N - (NT - 1) * P, NT - 1, :], a.x_in[(NT - 1) * P:N, :]).then_inc(sem("ldx"), 16)
            eng.dma_start(wl0[:, :, :], a.w0.rearrange("(c p) o -> p c o", p=P)).then_inc(sem("ld3"), 16)
            eng.dma_start(bc[:, 0, :], a.vecs[0:1, :].to_broadcast([P, D])).then_inc(sem("ld3"), 16)
            eng.wait_ge(sem("zero"), 1)
            eng.wait_ge(sem("win"), 48)
            tz = table.rearrange("(k p c) w -> k p (c w)", k=NT, p=P)

            def clear(k, s, r):
                if s or not isinstance(k, int):
                    eng.wait_ge(sem(f"ztab{1 - s}"), 16 * (r + 1 if s else r))
                    eng.sem_inc(sem("cleared"), 1)
                eng.dma_start(tz[bass.ds(k, 1), :, :].rearrange("a p c -> (a p) c"), zero).then_inc(sem(f"ztab{s}"), 16)
            skewed(eng, NT, clear)
            eng.wait_ge(sem("ztab0"), 16 * (NT - NT // 2))
            eng.sem_inc(sem("cleared"), 1)
            eng.wait_ge(sem("need"), 1)

            def load(k, s, r):
                eng.wait_ge(sem("tv"), 7 * k + 7)
                eng.wait_ge(sem("ta"), 7 * k + 7)
                if isinstance(k, int):
                    n = eng.value_load(need[0:1, k:k + 1], min_val=1, max_val=NGS)
                else:
                    n = eng.value_load(need[0:1, bass.ds(k, 1)], min_val=1, max_val=NGS)
                eng.wait_ge(sem("done"), n)
                eng.sem_inc(sem("pass"), 1)
                src_ap = tz[bass.ds(k, 1), :, :].rearrange("a p c -> (a p) c")
                eng.dma_start(tk[:, s, :, :, :].rearrange("p j d c -> p (j d c)"), src_ap).then_inc(sem(f"tk{s}"), 16)

            def store(k, s, r):
                one = lambda t: t[bass.ds(k, 1), :, :, :].rearrange("a p j d -> (a p) j d")
                eng.wait_ge(sem("cs"), k + 1)
                eng.dma_start(one(counts), cs).then_inc(sem("cs_out"), 16)
                col = lambda t: t[:, :, bass.ds(k, 1), :].rearrange("j p k s -> p (j k) s")
                eng.wait_ge(sem("tv"), 14 + 7 * k + 7)
                eng.dma_start(col(counts_t), ct).then_inc(sem("ct_out"), 16)
                eng.wait_ge(sem("ta"), 14 + 7 * k + 7)
                eng.dma_start(col(weights_t), wt).then_inc(sem("wt_out"), 16)
            skewed(eng, NT, load, store)
            for n in ("cs_out", "ct_out", "wt_out"):
                eng.wait_ge(sem(n), 16 * NT)

        @block.gpsimd
        def _(eng):
            n = [0]

            def do(ins):
                n[0] += 1
                ins.then_inc(sem("pool"), 1)
            eng.memset(zero, 0.0).then_inc(sem("zero"), 1)
            do(eng.memset(ident[:, :], 0.0))
            do(eng.memset(zbb[:, :], 0.0))
            do(eng.memset(sent, -1.0))
            do(eng.memset(eps[:, :], LN_EPS))
            do(eng.memset(rl[:, :, QB - 1, :], 0.0))
            do(eng.memset(hx[:, :, D:D + 1], 1.0))
            eng.memset(xs[:, NT - 1, :], 0.0).then_inc(sem("xpad"), 1)
            eng.wait_ge(sem("pool"), n[0])
            do(eng.affine_select(out=ident[:, :], in_=ident[:, :], compare_op=ALU.not_equal, fill=1.0,
                                 base=0, pattern=[[-1, P]], channel_multiplier=1))
            eng.wait_ge(sem("pool"), n[0])
            eng.tensor_copy(identb[:, :], ident[:, :]).then_inc(sem("const"), 1)
            blocks, inner = shifts(eng)
            with eng.Fori(0, blocks) as b:
                eng.wait_ge(sem("win"), 48 * b + 48)
                eng.sem_inc(sem("pass"), 1)
                with eng.Fori(0, inner) as i:
                    for s in range(2):
                        eng.wait_ge(sem("eqF"), (b * inner + i) * 2 + s + 1)
                        eng.sem_inc(sem("pass"), 1)
                        eng.tensor_tensor(wF[:, s, :], eqF[:, s, :], ewF[:, bass.ds(2 * i + s, EC)], ALU.mult)\
                           .then_inc(sem("wF"), 1)
                eng.drain()
                eng.sem_inc(sem("winfree"), 1)
            eng.wait_ge(sem("turned"), 1)

            def issue(g, s, r):
                tiles = eng.value_load(clr[0:1, g:g + 1] if isinstance(g, int) else clr[0:1, bass.ds(g, 1)],
                                       min_val=1, max_val=NT)
                eng.wait_ge(sem("cleared"), tiles)
                eng.sem_inc(sem("pass"), 1)
                eng.tensor_copy(idxs[:, s, :], idxT[:, bass.ds(GS * g, GS)]).then_inc(sem("stage"), 1)
                eng.tensor_copy(vals[:, s, :, :], valT[:, bass.ds(GS * g, GS), :]).then_inc(sem("stage"), 1)
                eng.wait_ge(sem("stage"), 2 * g + 2)
                eng.sem_inc(sem("pass"), 1)
                for c in range(GS):
                    eng.indirect_dma_start(out=table, out_offset=bass.IndirectOffsetOnAxis(idxs[:, s, c:c + 1], 0),
                                           in_=vals[:, s, c, :], in_offset=None, bounds_check=CELLS - 1,
                                           oob_is_err=False).then_inc(sem(f"scat{s}"), 16)

            def finish(g, s, r):
                eng.wait_ge(sem(f"scat{s}"), 16 * GS * (r + 1))
                eng.sem_inc(sem("done"), 1)
            skewed(eng, NGS, issue, finish)

        @block.vector
        def _(eng):
            ch = Chain(eng, sem("dve"))
            do, after = ch.do, ch.after
            eng.wait_ge(sem("ld"), 112)
            do(eng.tensor_scalar(t0, dsti, 7, None, ALU.logical_shift_right))
            do(eng.tensor_scalar(t1, dsti, 127, None, ALU.bitwise_and))
            after()
            do(eng.scalar_tensor_tensor(out=f0, in0=t0, scalar=float(P * NP), in1=t1, op0=ALU.mult, op1=ALU.add))
            after()
            do(eng.tensor_scalar(t0, srci, 7, None, ALU.logical_shift_right))
            do(eng.tensor_scalar(t1, srci, 127, None, ALU.bitwise_and))
            after()
            do(eng.scalar_tensor_tensor(out=f1, in0=t0, scalar=float(P), in1=f0, op0=ALU.mult, op1=ALU.add))
            after()
            do(eng.scalar_tensor_tensor(out=key, in0=t1, scalar=float(NP), in1=f1, op0=ALU.mult, op1=ALU.add))
            after()
            eng.wait_ge(sem("const"), 1)
            eng.sem_inc(sem("key"), 1)
            do(eng.tensor_tensor(f0, dsti, dst1, ALU.is_gt))
            after()
            do(eng.tensor_reduce(st[:, 0:1], f0, AX.X, ALU.max))
            do(eng.tensor_tensor(f1, dsti, dst1, ALU.is_equal))
            after()
            do(eng.tensor_tensor_scan(f0, f1, f1, 0.0, ALU.mult, ALU.add))
            after()
            do(eng.tensor_reduce(st[:, 1:2], f0, AX.X, ALU.max))
            do(eng.tensor_tensor(f1, dst2, dst3, ALU.is_equal))
            after()
            do(eng.tensor_tensor_scan(f0, f1, f1, 0.0, ALU.mult, ALU.add))
            after()
            do(eng.tensor_reduce(st[:, 2:3], f0, AX.X, ALU.max))
            after()
            do(eng.tensor_tensor(st[:, 3:4], st[:, 1:2], st[:, 2:3], ALU.max))
            after()
            do(eng.tensor_scalar(st[:, 6:7], st[:, 3:4], float(HALF - 1), None, ALU.is_ge))
            after()
            do(eng.tensor_tensor(st[:, 7:8], st[:, 6:7], st[:, 0:1], ALU.max))
            after()
            do(eng.scalar_tensor_tensor(out=st[:, 4:5], in0=st[:, 7:8], scalar=float(EP), in1=st[:, 3:4],
                                        op0=ALU.mult, op1=ALU.max))
            after()
            eng.sem_inc(sem("run"), 1)
            eng.wait_ge(sem("run_t"), 1)
            do(eng.tensor_reduce(st[0:1, 5:6], pg[0:1, 0:P], AX.X, ALU.max))
            after()
            do(eng.tensor_scalar(sti[0:1, 0:1], st[0:1, 5:6], 1.0, None, ALU.max))
            after()
            do(eng.tensor_scalar(sti[0:1, 1:2], sti[0:1, 0:1], float(SH - 1), None, ALU.add))
            do(eng.tensor_scalar(sti[0:1, 2:3], sti[0:1, 0:1], 1.0, float(SH), ALU.add, ALU.min))
            after()
            do(eng.tensor_scalar(sti[0:1, 1:2], sti[0:1, 1:2], 6, None, ALU.logical_shift_right))
            do(eng.tensor_scalar(sti[0:1, 2:3], sti[0:1, 2:3], 1, None, ALU.logical_shift_right))
            after()
            eng.sem_inc(sem("shift"), 1)
            do(eng.tensor_scalar(lastd[:, :], lastd[:, :], 7, None, ALU.logical_shift_right))
            do(eng.tensor_scalar(allclr[:, :], st[0:1, 5:6], float(EP), float(NT), ALU.is_ge, ALU.mult))
            after()
            do(eng.tensor_scalar(clr[:, :], lastd[:, :], 1.0, None, ALU.add))
            after()
            do(eng.tensor_tensor(clr[:, :], clr[:, :], allclr[:, 0:1].to_broadcast([1, NGS]), ALU.max))
            after()
            eng.sem_inc(sem("winfree"), 2)
            blocks, inner = shifts(eng)
            with eng.Fori(0, blocks) as b:
                with eng.Fori(0, inner) as i:
                    for s in range(2):
                        jj = 2 * i + s
                        eng.wait_ge(sem("win"), 48 * b + 48)
                        eng.wait_ge(sem("eqfree"), 2 * (b * inner + i) + s + 1)
                        eng.tensor_tensor(eqF[:, s, :], key, keyF[:, bass.ds(jj, EC)], ALU.is_equal).then_inc(sem("eqF"), 1)
                        eng.tensor_tensor(eqB[:, s, :], key, keyB[:, bass.ds(SH - 1 - jj, EC)], ALU.is_equal).then_inc(sem("eqB"), 1)
                eng.drain()
                eng.sem_inc(sem("winfree"), 1)
            eng.wait_ge(sem("sums"), 1)
            pv = lambda p: p[:, :, 0:HALF]
            hv = lambda t: t.rearrange("p (a c) -> p a c", a=2)
            do(eng.tensor_scalar(hv(cnt_e), pv(pc), 1.0, None, ALU.add))
            do(eng.tensor_tensor(hv(w_e), pv(pw), hv(ewt[:, :]), ALU.add))
            do(eng.tensor_scalar(hv(f0), pv(pd), 1.0, OUT_OF_TABLE, ALU.min, ALU.mult))
            after()
            do(eng.tensor_tensor(idx_e, f0, key, ALU.add))
            after()
            eng.sem_inc(sem("edges"), 1)
            do(eng.tensor_scalar(dst1, srci, 127, None, ALU.bitwise_and))
            do(eng.tensor_scalar(dsti, dsti, 7, None, ALU.logical_shift_right))
            do(eng.tensor_scalar(srci, srci, 7, None, ALU.logical_shift_right))
            after()
            do(eng.tensor_copy(lo, dst1))
            do(eng.tensor_copy(hi, srci))
            do(eng.tensor_copy(key, dsti))
            after()
            eng.wait_ge(sem("cols"), 1)
            for a0, b0, src_bank in ((0, 512, 0), (512, EC, 1)):
                w = b0 - a0
                do(eng.tensor_copy(idxT[:, a0:b0], pc[:, src_bank, 0:w]))
                do(eng.tensor_copy(valT[:, a0:b0, 0], pd[:, src_bank, 0:w]))
                do(eng.tensor_copy(valT[:, a0:b0, 1], pw[:, src_bank, 0:w]))
            after()
            eng.sem_inc(sem("turned"), 1)
            eng.wait_ge(sem("ld2"), 32)
            for k in range(NT):
                fs = (f0, f1)[k % 2]
                do(eng.scalar_tensor_tensor(out=fs, in0=key, scalar=float(k), in1=gno[:, :], op0=ALU.is_equal, op1=ALU.mult))
                after()
                do(eng.tensor_reduce(gm[:, k:k + 1], fs, AX.X, ALU.max))
            after()
            eng.sem_inc(sem("gm"), 1)
            eng.wait_ge(sem("gm_t"), 1)
            do(eng.tensor_reduce(gmax[:, :], pg[0:NT, 0:P], AX.X, ALU.max))
            after()
            do(eng.tensor_scalar(gmax[:, :], gmax[:, :], 1.0, None, ALU.max))
            after()
            eng.sem_inc(sem("gmax"), 1)
            eng.wait_ge(sem("gmax_t"), 1)
            do(eng.tensor_copy(need[:, :], pg[0:1, 256:256 + NT]))
            after()
            eng.sem_inc(sem("need"), 1)

            def onehot(g, s, r):
                cols = lambda t: t[:, bass.ds(G * g, G)].unsqueeze(2)
                if not (isinstance(g, int) and g == 0):
                    eng.wait_ge(sem("hfree"), g)
                eng.tensor_tensor(hlo[:, s, :, :], cols(lo).to_broadcast([P, G, P]),
                                  io[:, :].unsqueeze(1).to_broadcast([P, G, P]), ALU.is_equal).then_inc(sem("hot"), 1)
                do(eng.tensor_tensor(hhi[:, s, :, 0, :], cols(hi).to_broadcast([P, G, NT]),
                                     io[:, 0:NT].unsqueeze(1).to_broadcast([P, G, NT]), ALU.is_equal))
                after()
                eng.tensor_tensor(hhi[:, s, :, 1, :], hhi[:, s, :, 0, :],
                                  cols(ewt[:, :]).to_broadcast([P, G, NT]), ALU.mult).then_inc(sem("hot"), 1)
            ch.run(NG, 1, onehot)
            eng.wait_ge(sem("ldx"), 32)
            a.layernorm_stats(ch)
            a.aggregate_stats(ch)
            eng.wait_ge(sem("degr"), 1)
            eng.tensor_copy(sq[0:2 * NT, 0:P], phr).then_inc(sem("degc"), 1)
            eng.wait_ge(sem("deg"), 1)
            php = ph.rearrange("p (a n) -> p a n", a=2)
            do(eng.tensor_scalar(od2[:, 0, :], php[:, 0, :], 1.0, None, ALU.max))
            do(eng.tensor_scalar(od3[:, 1, :], php[:, 1, :], 1.0, None, ALU.add))
            after()
            do(eng.tensor_scalar(od2[:, 1, :], od3[:, 1, :], 1e-30, None, ALU.max))
            after()
            eng.sem_inc(sem("stat"), 1)
            eng.wait_ge(sem("stat_r"), 1)
            do(eng.reciprocal(rso[:, :], od3[:, 0, :]))
            do(eng.tensor_scalar(gm[:, :], od2[:, 1, :], 1e-30, None, ALU.is_gt))
            do(eng.reciprocal(dinv[:, :], od2[:, 0, :]))
            do(eng.reciprocal(rstd[:, :], shift[:, :]))
            after()
            do(eng.tensor_tensor(dinv[:, :], dinv[:, :], gm[:, :], ALU.mult))
            do(eng.scalar_tensor_tensor(out=shift[:, :], in0=mv[:, :, 0], scalar=-1.0, in1=rstd[:, :], op0=ALU.mult, op1=ALU.mult))
            after()
            do(eng.tensor_tensor(od3[:, 0, :], rstd[:, :], rso[:, :], ALU.mult))
            do(eng.tensor_tensor(od3[:, 1, :], shift[:, :], rso[:, :], ALU.mult))
            after()
            eng.sem_inc(sem("scaled"), 1)
            eng.wait_ge(sem("ld3"), 32)
            eng.sem_inc(sem("tv"), 14)
            eng.sem_inc(sem("ab"), 2)

            def tile(k, s, r):
                one = lambda t: t[:, bass.ds(k, 1)]
                eng.wait_ge(sem("q"), k + 1)
                eng.wait_ge(sem("abfree"), k + 1)
                do(eng.tensor_scalar(q[:, :], pq[:, s, 0:D], one(rso), None, ALU.mult))
                do(eng.tensor_scalar(msk[:, :], pq[:, s, D:D + 1], 0.0, None, ALU.is_gt))
                after()
                eng.wait_ge(sem("hk"), k + 1)
                do(eng.tensor_tensor(ab[:, 0, :], q[:, :], hk[:, :], ALU.add))
                after()
                eng.tensor_tensor(ab[:, 1, :], q[:, :], hk[:, :], ALU.mult).then_inc(sem("ab"), 1)
                for g in range(7):
                    w = min(4, NT - 4 * g)
                    eng.wait_ge(sem("tc"), 7 * k + g + 1)
                    if g == 0 and not (isinstance(k, int)):
                        eng.wait_ge(sem("ct_out"), 16 * k)
                    eng.tensor_copy(ct[:, 4 * g:4 * g + w, :].rearrange("p j s -> p (j s)"),
                                    ptc[:, (g + s) % 2, 0:w * P]).then_inc(sem("tv"), 1)
                eng.wait_ge(sem("e"), k + 1)
                do(eng.scalar_tensor_tensor(out=e1[:, :], in0=pe, scalar=msk[:, :], in1=bc[:, 0, :], op0=ALU.mult, op1=ALU.add))
                after()
                do(eng.scalar_tensor_tensor(out=e2[:, :], in0=e1[:, :], scalar=0.01, in1=e1[:, :], op0=ALU.mult, op1=ALU.max))
                after()
                eng.tensor_tensor_reduce(out=sq[:, :], in0=e2[:, :], in1=e2[:, :], scale=1.0, scalar=0.0,
                                         op0=ALU.mult, op1=ALU.add, accum_out=nrm[:, 0:1]).then_inc(sem("ss"), 1)
                eng.wait_ge(sem("root"), k + 1)
                do(eng.tensor_scalar(nrm[:, 2:3], nrm[:, 1:2], 1e-12, None, ALU.max))
                after()
                do(eng.reciprocal(nrm[:, 3:4], nrm[:, 2:3]))
                after()
                xk = xs[:, bass.ds(k, 1), :].rearrange("p a d -> p (a d)")
                do(eng.scalar_tensor_tensor(out=xk, in0=e2[:, :], scalar=nrm[:, 3:4], in1=xk, op0=ALU.mult, op1=ALU.add))
                after()
                a.tile_stats(ch, k)
            ch.run(NT, 9, tile)

        @block.scalar
        def _(eng):
            kf = lambda t: t.rearrange("(p c) -> p c", p=P)
            row = lambda t: t.rearrange("(p c) -> p c", p=1)
            eng.wait_ge(sem("const"), 1)
            eng.wait_ge(sem("ld"), 112)
            for d, t in ((keyflat[0:EP], sent), (keyflat[KF + EP:KF + 2 * EP], sent),
                         (ewflat[0:EP], ewt[:, :]), (ewflat[EP:2 * EP], sent)):
                eng.dma_start(kf(d), t).then_inc(sem("flat"), 16)
            for d in (keyflat[EP:KF], keyflat[KF + 2 * EP:2 * KF + EP], ewflat[2 * EP:EP + KF]):
                eng.dma_start(row(d), sent[0:1, :]).then_inc(sem("flat"), 16)
            eng.wait_ge(sem("key"), 1)
            eng.dma_start(kf(keyflat[KF:KF + EP]), key).then_inc(sem("flat"), 16)
            eng.wait_ge(sem("flat"), 128)
            blocks, inner = shifts(eng)
            with eng.Fori(0, blocks) as b:
                eng.wait_ge(sem("winfree"), 2 * b + 2)

                def window(t, off):
                    base = t[bass.ds(off, EP)].rearrange("(p c) -> p c", p=P)
                    return bass.AP(tensor=base.tensor, offset=base.offset, ap=[[EC, P], [1, W]])
                for tile, t, off in ((keyF, keyflat, KF + 1 + SH * b), (keyB, keyflat, KF - SH - SH * b),
                                     (ewF, ewflat, 1 + SH * b)):
                    eng.dma_start(tile, window(t, off)).then_inc(sem("win"), 16)
            eng.wait_ge(sem("edges"), 1)
            for n, t in enumerate((idx_e, cnt_e, w_e)):
                eng.dma_start(kf(turn[n, 0:EP]), t).then_inc(sem("turn_out"), 16)
            eng.wait_ge(sem("turn_out"), 48)
            for n in range(3):
                eng.dma_start(rl[:, n, 0:QB - 1, :], turn[n, 0:(QB - 1) * P * P].rearrange("(b q e) -> q b e", q=P, e=P)).then_inc(sem("turn_in"), 16)
                rest = EC - (QB - 1) * P
                eng.dma_start(rl[0:rest, n, QB - 1, :], turn[n, (QB - 1) * P * P:EP].rearrange("(q e) -> q e", e=P)).then_inc(sem("turn_in"), 16)
            eng.wait_ge(sem("stat"), 1)
            eng.activation(od3[:, 0, :], od2[:, 0, :], ACT.Sqrt).then_inc(sem("act"), 1)
            eng.activation(shift[:, :], mv[:, :, 1], ACT.Sqrt, bias=eps[:, :]).then_inc(sem("act"), 1)
            eng.wait_ge(sem("act"), 2)
            eng.activation(od2[:, 0, :], od2[:, 1, :], ACT.Sqrt).then_inc(sem("stat_r"), 1)
            eng.wait_ge(sem("scaled"), 1)
            for t in range(NT):
                last = eng.activation(hx[:, t, 0:D], xs[:, t, :], ACT.Relu, bias=od3[:, 1, t:t + 1], scale=od3[:, 0, t:t + 1])
            last.then_inc(sem("u"), 1)
            eng.sem_inc(sem("ta"), 14)
            eng.sem_inc(sem("abfree"), 1)

            def tile(k, s, r):
                one = lambda t: t[:, bass.ds(k, 1)]
                eng.wait_ge(sem(f"tk{s}"), 16 * r + 16)
                if not isinstance(k, int):
                    eng.wait_ge(sem("cs_out"), 16 * k)
                eng.activation(cs, tk[:, s, :, :, 0], ACT.Copy).then_inc(sem("cs"), 1)
                eng.wait_ge(sem("ab"), k + 2)
                eng.activation(hk[:, :], xs[:, bass.ds(k, 1), :].rearrange("p a d -> p (a d)"), ACT.Relu,
                               bias=one(shift), scale=one(rstd)).then_inc(sem("hk"), 1)
                for g in range(7):
                    w = min(4, NT - 4 * g)
                    eng.wait_ge(sem("tw"), 7 * k + g + 1)
                    if g == 0 and not isinstance(k, int):
                        eng.wait_ge(sem("wt_out"), 16 * k)
                    eng.activation(wt[:, 4 * g:4 * g + w, :].rearrange("p j s -> p (j s)"),
                                   ptw[:, (g + s) % 2, 0:w * P], ACT.Copy).then_inc(sem("ta"), 1)
                eng.wait_ge(sem("abt"), k + 1)
                eng.activation(abT[:, :, :].rearrange("p c n -> p (c n)"), pab, ACT.Copy).then_inc(sem("abfree"), 1)
                eng.wait_ge(sem("ss"), k + 1)
                eng.activation(nrm[:, 1:2], nrm[:, 0:1], ACT.Sqrt).then_inc(sem("root"), 1)
            skewed(eng, NT, tile)

        @block.tensor
        def _(eng):
            mm = lambda o, l, r_, st, sp: eng.matmul(o, l, r_, start=st, stop=sp, skip_group_check=True)
            eng.wait_ge(sem("const"), 1)

            def edge(st, sp):
                for h in range(2):
                    for t in (pc, pd, pw):
                        last = mm(t[:, h, :], identb[:, :], zbb[:, :], st, sp)
                return last
            edge(True, False).then_inc(sem("eqfree"), 2)
            eng.wait_ge(sem("run"), 1)
            eng.transpose(pg[0:1, 0:P], st[:, 4:5], ident[:, :]).then_inc(sem("run_t"), 1)
            blocks, inner = shifts(eng)
            with eng.Fori(0, blocks) as b:
                with eng.Fori(0, inner) as i:
                    for s in range(2):
                        eng.wait_ge(sem("wF"), (b * inner + i) * 2 + s + 1)
                        eng.wait_ge(sem("eqB"), (b * inner + i) * 2 + s + 1)
                        for h in range(2):
                            c = slice(h * HALF, (h + 1) * HALF)
                            mm(pc[:, h, 0:HALF], identb[:, :], eqF[:, s, c], False, False)
                            mm(pd[:, h, 0:HALF], identb[:, :], eqB[:, s, c], False, False)
                            last = mm(pw[:, h, 0:HALF], ident[:, :], wF[:, s, c], False, False)
                        last.then_inc(sem("eqfree"), 1)
            edge(False, True).then_inc(sem("sums"), 1)
            eng.wait_ge(sem("edges"), 1)
            eng.wait_ge(sem("turn_in"), 96)
            for n, t in enumerate((pc, pd, pw)):
                for b in range(QB):
                    last = eng.transpose(t[:, b // 4, (b % 4) * P:(b % 4 + 1) * P], rl[:, n, b, :], ident[:, :])
            last.then_inc(sem("cols"), 1)
            eng.wait_ge(sem("gm"), 1)
            eng.transpose(pg[0:NT, 0:P], gm[:, :], ident[:, :]).then_inc(sem("gm_t"), 1)
            eng.wait_ge(sem("gmax"), 1)
            eng.matmul(pg[0:1, 256:256 + NT], gmax[:, :], ident[0:NT, 0:NT], start=True, stop=True).then_inc(sem("gmax_t"), 1)
            mm(phr, identb[:, 0:2 * NT], zbb[:, 0:P], True, False).then_inc(sem("hfree"), 1)

            def degrees(g, s, r):
                eng.wait_ge(sem("hot"), 2 * g + 2)
                for c in range(G):
                    last = mm(phr, hhi[:, s, c, :, :].rearrange("p a n -> p (a n)"), hlo[:, s, c, :], False, False)
                last.then_inc(sem("hfree"), 1)
            skewed(eng, NG, degrees)
            mm(phr, identb[:, 0:2 * NT], zbb[:, 0:P], False, True).then_inc(sem("degr"), 1)
            eng.wait_ge(sem("degc"), 1)
            eng.transpose(ph, sq[0:2 * NT, 0:P], ident[0:2 * NT, 0:2 * NT]).then_inc(sem("deg"), 1)
            eng.wait_ge(sem("u"), 1)
            eng.wait_ge(sem("ld3"), 32)

            def tile(k, s, r):
                eng.wait_ge(sem(f"tk{s}"), 16 * r + 16)
                eng.wait_ge(sem("ab"), k + 1)
                for j in range(NT):
                    last = eng.matmul(pq[:, s, 0:D + 1], tk[:, s, j, :, 0], hx[:, j, :], start=j == 0, stop=j == NT - 1)
                last.then_inc(sem("q"), 1)
                for g in range(7):
                    for c, bank, free, ready in ((0, ptc, "tv", "tc"), (1, ptw, "ta", "tw")):
                        eng.wait_ge(sem(free), 7 * k + g + 13)
                        for j in range(4 * g, min(NT, 4 * g + 4)):
                            o = (j - 4 * g) * P
                            last = eng.transpose(bank[:, (g + s) % 2, o:o + P], tk[:, s, j, :, c], ident[:, :])
                        last.then_inc(sem(ready), 1)
                eng.wait_ge(sem("ab"), k + 3)
                for c in range(4):
                    last = eng.transpose(pab[:, c * P:(c + 1) * P], ab[:, c // 2, (c % 2) * P:(c % 2 + 1) * P], ident[:, :])
                last.then_inc(sem("abt"), 1)
                eng.wait_ge(sem("abfree"), k + 2)
                for c in range(4):
                    last = eng.matmul(pe, abT[:, c, :], wl0[:, c, :], start=c == 0, stop=c == 3)
                last.then_inc(sem("e"), 1)
            skewed(eng, NT, tile)

PARTS = [range(0, 7), range(7, 13), range(13, 19), range(19, NT)]


def phase_l1(nc, sem, sb, a):
    psum, xs, hx, ident, dinv = a.psum, a.xs, a.hx, a.ident, a.dinv
    with ExitStack() as ctx:
        def buf(name, shape, dt=F32):
            return sb(name, shape, dt, ctx)
        s_ = lambda n: sem("l1_" + n)
        wt = buf("l1wt", [P, 2, NT, P])
        w = buf("l1w", [P, 6, D])
        col = buf("l1col", [P, 4])
        b2 = buf("l1b2", [P, D])
        g1, g2 = buf("g1", [P, D]), buf("g2", [P, D])
        gT, h7T, hT = (buf(n, [P, 2, P]) for n in ("gT", "h7T", "hT"))
        res = buf("l1res", [P, D])
        pq, pA, pB, pC, pD = psum[:, 0:2, 0:D], psum[:, 2, 0:D], psum[:, 3, 0:D], psum[:, 4, 0:D], psum[:, 5, 0:D]
        block = ctx.enter_context(nc.Block())

        @block.sync
        def _(eng):
            eng.dma_start(w[:, :, :], a.w1.rearrange("(c p) o -> p c o", p=P)).then_inc(s_("par"), 16)
            eng.dma_start(col[:, :], a.cols).then_inc(s_("par"), 16)
            eng.dma_start(b2[:, :], a.vecs[1:2, :].to_broadcast([P, D])).then_inc(s_("par"), 16)

            def load(k, s, r):
                if not isinstance(k, int):
                    eng.wait_ge(s_("q"), k)
                eng.dma_start(wt[:, s, :, :], a.weights_t.ap()[bass.ds(k, 1), :, :, :].rearrange("a p k s -> (a p) k s"))\
                   .then_inc(s_(f"wt{s}"), 16)
            skewed(eng, NT, load)

        @block.tensor
        def _(eng):
            eng.sem_inc(s_("q"), 1)
            eng.wait_ge(s_("par"), 48)
            mm = eng.matmul

            def step(cur, prev):
                def part(n):
                    if cur:
                        k, s, r = cur
                        if n == 0:
                            eng.wait_ge(s_(f"wt{s}"), 16 * r + 16)
                        for t in PARTS[n]:
                            last = mm(pq[:, s, :], wt[:, s, t, :], hx[:, t, 0:D], start=t == 0, stop=t == NT - 1)
                        if n == 3:
                            last.then_inc(s_("q"), 1)
                part(0)
                if prev:
                    k = prev[0]
                    eng.wait_ge(s_("g"), k + 1)
                    for c in range(2):
                        last = eng.transpose(pA[:, c * P:(c + 1) * P], g2[:, c * P:(c + 1) * P], ident[:, :])
                    last.then_inc(s_("A"), 1)
                part(1)

                def dense(ready, w0, rhs, ps, done):
                    if prev:
                        eng.wait_ge(s_(ready), k + 1)
                        for m in range(2):
                            for c in range(2):
                                last = mm(ps[:, m * P:(m + 1) * P], w[:, w0 + c, m * P:(m + 1) * P], rhs[:, c, :],
                                          start=c == 0, stop=c == 1)
                        last.then_inc(s_(done), 1)
                dense("gT", 0, gT, pB, "B")
                part(2)
                dense("h7T", 2, h7T, pC, "C")
                part(3)
                if prev:
                    eng.wait_ge(s_("hT"), k + 1)
                    eng.wait_ge(s_("x"), k + 1)
                    for c in range(2):
                        last = mm(pD, hT[:, c, :], w[:, 4 + c, :], start=c == 0, stop=c == 1)
                    last.then_inc(s_("D"), 1)
            overlapped(eng, NT, step)

        @block.scalar
        def _(eng):
            def tile(k, s, r):
                eng.wait_ge(s_("A"), k + 1)
                eng.activation(gT[:, :, :].rearrange("p c n -> p (c n)"), pA, ACT.Copy).then_inc(s_("gT"), 1)
                eng.wait_ge(s_("B"), k + 1)
                eng.activation(h7T[:, 0, :], pB[:, 0:P], ACT.Identity, bias=col[:, 0:1])
                eng.activation(h7T[:, 1, :], pB[:, P:D], ACT.Identity, bias=col[:, 1:2]).then_inc(s_("h7T"), 1)
                eng.wait_ge(s_("C"), k + 1)
                eng.activation(hT[:, 0, :], pC[:, 0:P], ACT.Relu, bias=col[:, 2:3])
                eng.activation(hT[:, 1, :], pC[:, P:D], ACT.Relu, bias=col[:, 3:4]).then_inc(s_("hT"), 1)
            eng.wait_ge(s_("par"), 48)
            skewed(eng, NT, tile)

        @block.vector
        def _(eng):
            ch, ch2 = Chain(eng, s_("dve")), Chain(eng, s_("dve2"))
            eng.wait_ge(s_("par"), 48)
            eng.sem_inc(s_("x"), 1)

            def main(k, s, r):
                eng.wait_ge(s_("q"), k + 2)
                eng.tensor_tensor(g1[:, :], pq[:, s, :], hx[:, bass.ds(k, 1), 0:D].rearrange("p a d -> p (a d)"), ALU.add).then_inc(s_("g1"), 1)
                eng.wait_ge(s_("g1"), k + 1)
                eng.tensor_scalar(g2[:, :], g1[:, :], dinv[:, bass.ds(k, 1)], None, ALU.mult).then_inc(s_("g"), 1)

            def late3(k, s, r):
                ch.n, ch.rounds = 0, 2 * k
                eng.wait_ge(s_("D"), k + 1)
                xk = xs[:, bass.ds(k, 1), :].rearrange("p a d -> p (a d)")
                eng.tensor_tensor(res[:, :], pD, b2[:, :], ALU.add).then_inc(s_("x"), 1)
                eng.wait_ge(s_("x"), k + 2)
                ch.do(eng.tensor_tensor(xk, xk, res[:, :], ALU.add))
                ch.after()
                a.tile_stats(ch, k)
                assert ch.n == 2
            skewed(eng, NT, main, late3)


def phase_l2(nc, sem, sb, a):
    psum, xs, hx, ident = a.psum, a.xs, a.hx, a.ident
    with ExitStack() as ctx:
        def buf(name, shape, dt=F32):
            return sb(name, shape, dt, ctx)
        s_ = lambda n: sem("l2_" + n)
        ca, cb = buf("ca", [P, 2, NT, P]), buf("cb", [P, 2, NT, P])
        ys = buf("ys", [P, NT, D])
        w = buf("l2w", [P, 4, D])
        bc = buf("l2bc", [P, 4, D])
        q = buf("l2q", [P, D + 1])
        aT = buf("l2aT", [P, 4, P])
        y1 = buf("y1", [P, D])
        rsk = buf("rsk", [P, 2])
        sq = buf("l2sq", [P, 2, D])
        ones = buf("ones", [P, 2, P])
        mean, var, sd, A = (buf(n, [P, D]) for n in ("l2mean", "l2var", "l2sd", "l2A"))
        pq, pA, pY, pM, pV = psum[:, 0:2, 0:D + 1], psum[:, 2, :], psum[:, 3, 0:D], psum[:, 4, 0:D], psum[:, 5, 0:D]
        REAL = N - (NT - 1) * P
        block = ctx.enter_context(nc.Block())

        @block.sync
        def _(eng):
            eng.dma_start(w[:, :, :], a.w2.rearrange("(c p) o -> p c o", p=P)).then_inc(s_("par"), 16)
            for n in range(4):
                eng.dma_start(bc[:, n, :], a.vecs[2 + n:3 + n, :].to_broadcast([P, D])).then_inc(s_("par"), 16)

            def load(k, s, r):
                if not isinstance(k, int):
                    eng.wait_ge(s_("q"), k)
                for t, d in ((ca, a.counts), (cb, a.counts_t)):
                    eng.dma_start(t[:, s, :, :], d.ap()[bass.ds(k, 1), :, :, :].rearrange("a p k s -> (a p) k s"))\
                       .then_inc(s_(f"c{s}"), 16)
            skewed(eng, NT, load)

        @block.gpsimd
        def _(eng):
            eng.memset(ones[:, :, :], 1.0).then_inc(s_("ones0"), 1)
            eng.wait_ge(s_("ones0"), 1)
            eng.affine_select(out=ones[:, 1, :], in_=ones[:, 1, :], compare_op=ALU.is_gt, fill=0.0,
                              base=REAL, pattern=[[0, P]], channel_multiplier=-1).then_inc(s_("ones"), 1)

        @block.tensor
        def _(eng):
            eng.sem_inc(s_("q"), 1)
            eng.wait_ge(s_("par"), 80)
            mm = eng.matmul

            def step(cur, prev):
                def part(n):
                    if cur:
                        k, s, r = cur
                        if n == 0:
                            eng.wait_ge(s_("sum"), k + 1)
                        for t in PARTS[n]:
                            last = mm(pq[:, s, :], ca[:, s, t, :], hx[:, t, :], start=t == 0, stop=t == NT - 1)
                        if n == 3:
                            last.then_inc(s_("q"), 1)
                part(0)
                part(1)
                if prev:
                    k = prev[0]
                    eng.wait_ge(s_("g"), k + 1)
                    for c in range(2):
                        last = eng.transpose(pA[:, c * P:(c + 1) * P], y1[:, c * P:(c + 1) * P], ident[:, :])
                    for c in range(2):
                        last = eng.transpose(pA[:, (2 + c) * P:(3 + c) * P], q[:, c * P:(c + 1) * P], ident[:, :])
                    last.then_inc(s_("A"), 1)
                part(2)
                part(3)
                if prev:
                    eng.wait_ge(s_("aT"), k + 1)
                    eng.wait_ge(s_("y"), k + 1)
                    for c in range(4):
                        last = mm(pY, aT[:, c, :], w[:, c, :], start=c == 0, stop=c == 3)
                    last.then_inc(s_("Y"), 1)
            overlapped(eng, NT, step)
            eng.wait_ge(s_("ones"), 1)
            eng.wait_ge(s_("y"), NT + 1)
            for t in range(NT):
                last = mm(pM, ones[:, t // (NT - 1), :], ys[:, t, :], start=t == 0, stop=t == NT - 1)
            last.then_inc(s_("mean"), 1)

            def square(k, s, r):
                eng.wait_ge(s_("sq"), k + 1)
                o = 1 if isinstance(k, int) and k == NT - 1 else 0
                mm(pV, ones[:, o, :], sq[:, s, :], start=isinstance(k, int) and k == 0, stop=o == 1,
                   skip_group_check=True).then_inc(s_("sqfree"), 1)
            square(0, 0, 0)
            with eng.Fori(0, NT // 2 - 1) as i:
                square(2 * i + 1, 1, i)
                square(2 * i + 2, 0, i)
            square(NT - 2, 1, 0)
            square(NT - 1, 0, 0)

        @block.scalar
        def _(eng):
            def tile(k, s, r):
                eng.wait_ge(s_("A"), k + 1)
                eng.activation(aT[:, :, :].rearrange("p c n -> p (c n)"), pA, ACT.Copy).then_inc(s_("aT"), 1)
            skewed(eng, NT, tile)
            eng.wait_ge(s_("cent"), 1)
            eng.sem_inc(s_("sqfree"), 2)

            def square(k, s, r):
                eng.wait_ge(s_("sqfree"), k + 1)
                eng.activation(sq[:, s, :], ys[:, bass.ds(k, 1), :].rearrange("p a d -> p (a d)"), ACT.Square).then_inc(s_("sq"), 1)
            skewed(eng, NT, square)
            eng.wait_ge(s_("var"), 1)
            eng.activation(sd[:, :], var[:, :], ACT.Sqrt, bias=a.eps[:, :]).then_inc(s_("sd"), 1)

        @block.vector
        def _(eng):
            eng.wait_ge(s_("par"), 80)
            eng.sem_inc(s_("y"), 1)

            def add(k, s, r):
                eng.wait_ge(s_(f"c{s}"), 32 * r + 32)
                eng.tensor_tensor(ca[:, s, :, :], ca[:, s, :, :], cb[:, s, :, :], ALU.add).then_inc(s_("sum"), 1)

            def take(k, s, r):
                eng.wait_ge(s_("q"), k + 2)
                eng.tensor_copy(y1[:, :], hx[:, bass.ds(k, 1), 0:D].rearrange("p a d -> p (a d)"))
                eng.tensor_copy(q[:, :], pq[:, s, :]).then_inc(s_("g"), 1)

            def late(k, s, r):
                eng.wait_ge(s_("Y"), k + 1)
                yk = ys[:, bass.ds(k, 1), :].rearrange("p a d -> p (a d)")
                eng.tensor_tensor(yk, pY, bc[:, 0, :], ALU.add).then_inc(s_("y0"), 1)
                eng.wait_ge(s_("y0"), k + 1)
                eng.scalar_tensor_tensor(out=yk, in0=bc[:, 1, :], scalar=rsk[:, s:s + 1], in1=yk,
                                         op0=ALU.mult, op1=ALU.add).then_inc(s_("y"), 1)

            def take2(k, s, r):
                take(k, s, r)
                if not (isinstance(k, int) and k == 0):
                    eng.wait_ge(s_("y"), k)
                eng.tensor_copy(rsk[:, s:s + 1], pq[:, s, D:D + 1]).then_inc(s_("rs"), 1)

            def late2(k, s, r):
                eng.wait_ge(s_("rs"), k + 1)
                late(k, s, r)
            add(0, 0, 0)
            add(1, 1, 0)
            take2(0, 0, 0)
            with eng.Fori(0, NT // 2 - 1) as i:
                add(2 * i + 2, 0, i + 1)
                take2(2 * i + 1, 1, i)
                late2(2 * i, 0, i)
                add(2 * i + 3, 1, i + 1)
                take2(2 * i + 2, 0, i + 1)
                late2(2 * i + 1, 1, i)
            add(NT - 1, 0, NT // 2)
            take2(NT - 2, 1, NT // 2 - 1)
            late2(NT - 3, 0, NT // 2 - 1)
            take2(NT - 1, 0, NT // 2)
            late2(NT - 2, 1, NT // 2 - 1)
            late2(NT - 1, 0, NT // 2)
            ch = Chain(eng, s_("dve"))
            do, after = ch.do, ch.after
            wide = lambda t: t[:, :].unsqueeze(1).to_broadcast([P, NT, D])
            eng.wait_ge(s_("mean"), 1)
            do(eng.tensor_scalar(mean[:, :], pM, 1.0 / N, None, ALU.mult))
            after()
            do(eng.tensor_tensor(ys[:, :, :], ys[:, :, :], wide(mean), ALU.subtract))
            after()
            eng.sem_inc(s_("cent"), 1)
            eng.wait_ge(s_("sqfree"), NT + 2)
            do(eng.tensor_scalar(var[:, :], pV, 1.0 / N, None, ALU.mult))
            after()
            eng.sem_inc(s_("var"), 1)
            eng.wait_ge(s_("sd"), 1)
            do(eng.reciprocal(A[:, :], sd[:, :]))
            after()
            do(eng.tensor_tensor(A[:, :], A[:, :], bc[:, 2, :], ALU.mult))
            after()
            do(eng.tensor_tensor(ys[:, :, :], ys[:, :, :], wide(A), ALU.mult))
            after()
            do(eng.tensor_tensor(ys[:, :, :], ys[:, :, :], bc[:, 3:4, :].to_broadcast([P, NT, D]), ALU.add))
            after()
            do(eng.scalar_tensor_tensor(out=xs[:, :, :], in0=ys[:, :, :], scalar=0.0, in1=xs[:, :, :], op0=ALU.max, op1=ALU.add))
            after()
            a.layernorm_stats(ch)


BIG = 3.0e38
TAIL_SEMS = ("neg", "elu", "pos", "x", "out")
SPREAD = 80.0
H = 4
HD = D // H
FW = HD + 1
PB = 7


def ring4(eng, step):
    assert NT % 4 == 1
    step((0, 0, 0), None)
    with eng.Fori(0, NT // 4) as i:
        for u in range(1, 5):
            step((4 * i + u, u % 4, 2 * i + u // 2), (4 * i + u - 1, u - 1, 2 * i + (u - 1) // 2))
    step(None, (NT - 1, 0, NT // 2))


def heads(eng, body):
    with eng.Fori(0, H // 2) as i:
        for u in range(2):
            body(2 * i + u, u, i)


def to_rows(eng, src, ident, dst_ps, ready, took):
    for g in range(7):
        eng.wait_ge(took, g + 1)
        for t in range(4 * g, min(NT, 4 * g + 4)):
            last = eng.transpose(dst_ps[0:2 * H, g % 2, (t - 4 * g) * P:(t - 4 * g + 1) * P], src[:, t, :], ident[:, :])
        last.then_inc(ready, 1)

def take_rows(eng, dst_sb, src_ps, ready, took):
    eng.sem_inc(took, 2)
    for g in range(7):
        w = min(4, NT - 4 * g) * P
        eng.wait_ge(ready, g + 1)
        eng.tensor_copy(dst_sb[:, 4 * g * P:4 * g * P + w], src_ps[0:2 * H, g % 2, 0:w]).then_inc(took, 1)


def phase_l3(nc, sem, sb, a):
    psum, xs, hx, ident = a.psum, a.xs, a.hx, a.ident
    s_ = lambda n: sem("l3_" + n)
    flat2 = lambda t: t.rearrange("p a d -> p (a d)")
    with ExitStack() as outer:
        ftx = sb("ftx", [P, NT, H, FW], F32, outer)
        sc = sb("sc", [P, NT, 2 * H], F32, outer)
        sc02 = sb("sc02", [P, NT, 2 * H], F32, outer)
        rr = sb("rr", [P, NT, 2 * H], F32, outer)
        edge, edges = sb("edge", [P, 3 * H], F32, outer), sb("edges", [P, 3 * H], F32, outer)
        far, wide = sb("far", [P, 2 * H], F32, outer), sb("wide", [P, 1], F32, outer)
        wide_i = sb("wide_i", [P, 1], I32, outer)

        with ExitStack() as ctx:
            def buf(name, shape, dt=F32):
                return sb(name, shape, dt, ctx)
            w = buf("l3w", [P, 2, D + 2 * H])
            at = buf("l3at", [P, 2, D])
            prod = buf("l3prod", [P, 2, D])
            hT = buf("l3hT", [P, 2, 2, P])
            pT, pF = psum[:, 0:2, 0:D], psum[:, 2:4, 0:D + 2 * H]
            block = ctx.enter_context(nc.Block())

            @block.gpsimd
            def _(eng):
                eng.wait_ge(s_("edge"), 1)
                eng.partition_all_reduce(edges[:, :], edge[:, :], P, bass.bass_isa.ReduceOp.max).then_inc(s_("edges"), 1)

            @block.sync
            def _(eng):
                eng.dma_start(w[:, :, 0:D], a.w3.rearrange("(c p) o -> p c o", p=P)).then_inc(s_("par"), 16)
                for n in range(2):
                    eng.dma_start(at[:, n, :], a.vecs[6 + n:7 + n, :].to_broadcast([P, D])).then_inc(s_("par"), 16)

            @block.vector
            def _(eng):
                ch = Chain(eng, s_("dve"))
                eng.wait_ge(s_("par"), 48)
                for n in range(2):
                    ch.do(eng.tensor_tensor(prod[:, :, :], w[:, :, 0:D], at[:, n:n + 1, :].to_broadcast([P, 2, D]), ALU.mult))
                    ch.after()
                    ch.do(eng.tensor_reduce(w[:, :, D + H * n:D + H * n + H],
                                            prod[:, :, :].rearrange("p c (h d) -> p c h d", h=H), AX.X, ALU.add))
                    ch.after()
                ch.do(eng.memset(ftx[:, :, :, HD:FW], 1.0))
                ch.after()
                eng.sem_inc(s_("w"), 1)

                eng.wait_ge(s_("sc"), NT)
                ch.do(eng.tensor_scalar(sc02[:, :, :], sc[:, :, :], -1.0, None, ALU.mult))
                ch.after()
                by_head = lambda t, h0, n: t[:, :, h0:h0 + n].rearrange("p t h -> p h t")
                ch.do(eng.tensor_reduce(edge[:, 0:H], by_head(sc, 0, H), AX.X, ALU.max))
                ch.do(eng.tensor_reduce(edge[:, H:3 * H], by_head(sc02, 0, 2 * H), AX.X, ALU.max))
                ch.after()
                eng.sem_inc(s_("edge"), 1)
                ch.do(eng.tensor_scalar(sc02[:, :, :], sc[:, :, :], 0.2, None, ALU.mult))
                eng.wait_ge(s_("edges"), 1)
                ch.do(eng.tensor_tensor(far[:, 0:H], edges[:, 0:H], edges[:, H:2 * H], ALU.add))
                ch.do(eng.tensor_tensor(far[:, H:2 * H], edges[:, 2 * H:3 * H], edges[:, 0:H], ALU.subtract))
                ch.after()
                ch.do(eng.tensor_reduce(wide[:, :], far[:, :], AX.X, ALU.max))
                ch.after()
                ch.do(eng.tensor_scalar(wide_i[:, :], wide[:, :], SPREAD, None, ALU.is_gt))

            @block.scalar
            def _(eng):
                def evac(k, s, r):
                    eng.wait_ge(s_("T"), k + 1)
                    eng.activation(flat2(hT[:, s, :, :]), pT[:, s, :], ACT.Copy).then_inc(s_("hT"), 1)

                def feats(k, s, r):
                    eng.wait_ge(s_("F"), k + 1)
                    eng.activation(ftx[:, bass.ds(k, 1), :, 0:HD].rearrange("p a h d -> p (a h) d"),
                                   pF[:, s, 0:D].rearrange("p (h d) -> p h d", h=H), ACT.Copy).then_inc(s_("ft"), 1)
                    eng.activation(flat2(sc[:, bass.ds(k, 1), :]), pF[:, s, D:D + 2 * H], ACT.Copy).then_inc(s_("sc"), 1)
                eng.sem_inc(s_("ft"), 2)
                eng.wait_ge(s_("w"), 1)
                skewed(eng, NT, evac, feats)

            def product(eng, k):
                s = k % 2
                eng.wait_ge(s_("hT"), k + 1)
                eng.wait_ge(s_("ft"), k + 1)
                if k > 1:
                    eng.wait_ge(s_("sc"), k - 1)
                for c in range(2):
                    last = eng.matmul(pF[:, s, :], hT[:, s, c, :], w[:, c, :], start=c == 0, stop=c == 1)
                last.then_inc(s_("F"), 1)

            @block.tensor
            def _(eng):
                eng.wait_ge(s_("w"), 1)

                for k in range(NT):
                    s = k % 2
                    for c in range(2):
                        last = eng.transpose(pT[:, s, c * P:(c + 1) * P], hx[:, k, c * P:(c + 1) * P], ident[:, :])
                    last.then_inc(s_("T"), 1)
                    if k:
                        product(eng, k - 1)
                product(eng, NT - 1)

        for n in TAIL_SEMS:
            sem("l3t_" + n)
        spread = nc.values_load(wide_i[0:1, 0:1], min_val=0, max_val=1)
        with nc.If(spread == 0):
            with ExitStack() as ctx:
                l3_fast(nc, lender(nc, ctx), sb, ctx, a, ftx, sc, edges, rr)
        with nc.Else():
            with ExitStack() as ctx:
                l3_general(nc, lender(nc, ctx), sb, a, ftx, sc, sc02, rr)


def lender(nc, ctx):
    sems = {}

    def sem(name):
        if name not in sems:
            sems[name] = ctx.enter_context(nc.semaphore(name))
        return sems[name]
    return sem


def l3_fast(nc, sem, sb, outer, a, ftx, sc, edges, rr):
    psum, hx, ident = a.psum, a.hx, a.ident
    rrows = nc.dram_tensor("ratio_rows", [2 * H, NP], F32)
    s_ = lambda n: sem("l3f_" + n)
    flat2 = lambda t: t.rearrange("p a d -> p (a d)")
    e1, ne1, e2 = (sb(n, [P, NT, H], F32, outer) for n in ("e1s", "ne1s", "e2s"))
    with ExitStack() as ctx:
        rsb = sb("ratio_sb", [2 * H, NP], F32, ctx)
        pR = psum[:, 4:6, :]
        block = ctx.enter_context(nc.Block())

        @block.vector
        def _(eng):
            G_ = edges[:, 0:H].unsqueeze(1).to_broadcast([P, NT, H])
            ch = Chain(eng, s_("dve"))
            ch.do(eng.tensor_tensor(rr[:, :, 0:H], sc[:, :, 0:H], G_, ALU.subtract))
            ch.do(eng.tensor_tensor(rr[:, :, H:2 * H], sc[:, :, H:2 * H], G_, ALU.add))
            ch.after()
            eng.sem_inc(s_("z"), 1)
            eng.wait_ge(s_("exp"), 3)
            ch.do(eng.tensor_scalar(ne1[:, :, :], e1[:, :, :], -1.0, None, ALU.mult))
            take_rows(eng, rsb, pR, s_("ready"), s_("took"))

        @block.scalar
        def _(eng):
            eng.wait_ge(s_("z"), 1)
            eng.activation(e1[:, :, :], rr[:, :, 0:H], ACT.Exp).then_inc(s_("exp"), 1)
            eng.activation(e2[:, :, :], rr[:, :, 0:H], ACT.Exp, scale=0.2).then_inc(s_("exp"), 1)
            eng.activation(rr[:, :, H:2 * H], rr[:, :, H:2 * H], ACT.Exp, scale=-0.8).then_inc(s_("exp"), 1)

        @block.tensor
        def _(eng):
            eng.wait_ge(s_("exp"), 3)
            to_rows(eng, rr, ident, pR, s_("ready"), s_("took"))

        @block.sync
        def _(eng):
            eng.wait_ge(s_("took"), 2 + 7)
            eng.dma_start(rrows.ap(), rsb[:, :]).then_inc(s_("rrows"), 16)
            eng.wait_ge(s_("rrows"), 16)

    with ExitStack() as ctx:
        def buf(name, shape, dt=F32):
            return sb(name, shape, dt, ctx)
        halves = ((0, NT // 2), (NT // 2, NT - NT // 2))
        most = halves[1][1]
        rb = buf("ratio", [P, 2, NP])
        wgt = buf("wgt", [P, 2, 2, most * P])
        cj = buf("fcj", [P, 2, most, P])
        ft = buf("fft", [P, 2, 2, FW])
        oT = buf("oT", [P, 2, most * P])
        den, rden = buf("fden", [P, 2, most]), buf("frden", [P, 2, most])
        o = hx[:, :, 0:D]
        acc = [psum[:, 4 * u:4 * u + 4, :] for u in range(2)]
        BANK = 512
        block = ctx.enter_context(nc.Block())

        def passes(eng, step, before=None, after=None):
            with eng.Fori(0, H // 2) as i:
                if before:
                    before(i)
                for half in range(2):
                    g = 2 * i + half
                    overlapped(eng, NT, lambda cur, prev: cur and step(i, half, g, *cur))
                    if after:
                        after(i, half, g)

        def of_head(t, k, i, u):
            return flat2(t[:, bass.ds(k, 1), bass.ds(2 * i + u, 1)])

        @block.sync
        def _(eng):
            def ratios(i):
                eng.wait_ge(s_("t"), 4 * NT * i + 1)
                for u in range(2):
                    eng.dma_start(rb[:, u, :], rrows.ap()[bass.ds(2 * i + (H + u), 1), :].to_broadcast([P, NP]))\
                       .then_inc(s_("rb"), 16)

            def load(i, half, g, k, s, r):
                first = isinstance(k, int)
                t0, nt = halves[half]
                eng.wait_ge(s_("w"), 2 * NT * g + 2 * k + (2 if first else 0))
                eng.dma_start(cj[:, s, 0:nt, :], a.counts.ap()[t0:t0 + nt, :, bass.ds(k, 1), :].rearrange("k p j d -> p (k j) d"))\
                   .then_inc(s_(f"cj{s}"), 16)
            passes(eng, load, before=ratios)

        @block.gpsimd
        def _(eng):
            def stage(i, half, g, k, s, r):
                first = isinstance(k, int)
                eng.wait_ge(s_("m"), 2 * NT * g + (4 if first else 2 * k + 2))
                eng.sem_inc(s_("pass"), 1)
                eng.tensor_copy(ft[:, s, :, :], ftx[:, bass.ds(k, 1), bass.ds(2 * i, 2), :].rearrange("p a h d -> p (a h) d"))\
                   .then_inc(s_("ft"), 1)
            passes(eng, stage)

        def take_sums(eng, copy, u, half, g):
            n = halves[half][1] * P
            eng.wait_ge(s_("m"), 2 * NT * g + 2 * NT + 4)
            eng.sem_inc(s_("pass"), 1)
            copy(oT[0:FW, u, 0:n], acc[u][0:FW, :, :].rearrange("p b n -> p (b n)")[:, 0:n]).then_inc(s_("oT"), 1)

        @block.scalar
        def _(eng):
            eng.sem_inc(s_("t"), 1)

            def weights(i, half, g, k, s, r):
                t0, nt = halves[half]
                for u in range(2):
                    first = isinstance(k, int)
                    eng.wait_ge(s_("m"), 2 * NT * g + (4 if first else 2 * k + u + 1))
                    eng.wait_ge(s_("rb"), 32 * i + 32)
                    eng.sem_inc(s_("pass"), 1)
                    eng.activation(wgt[:, s, u, 0:nt * P], rb[:, u, t0 * P:(t0 + nt) * P], ACT.Relu,
                                   scale=of_head(e2, k, i, u), bias=of_head(ne1, k, i, u)).then_inc(s_("t"), 1)
            passes(eng, weights, after=lambda i, half, g: take_sums(
                eng, lambda to, what: eng.activation(to, what, ACT.Copy), 1, half, g))

        @block.vector
        def _(eng):
            eng.sem_inc(s_("w"), 2)
            eng.sem_inc(s_("ev"), 1)

            def count(i, half, g, k, s, r):
                nt = halves[half][1]
                loads = (NT - NT // 2, NT // 2)[s]
                for u in range(2):
                    eng.wait_ge(s_(f"cj{s}"), 16 * (loads * g + r + 1))
                    eng.wait_ge(s_("t"), 2 * NT * g + 2 * k + u + 2)
                    eng.scalar_tensor_tensor(out=wgt[:, s, u, 0:nt * P], in0=wgt[:, s, u, 0:nt * P],
                                             scalar=of_head(e1, k, i, u),
                                             in1=cj[:, s, 0:nt, :].rearrange("p k d -> p (k d)"),
                                             op0=ALU.add, op1=ALU.mult).then_inc(s_("w"), 1)

            def divide(i, half, g):
                t0, nt = halves[half]
                take_sums(eng, eng.tensor_copy, 0, half, g)
                eng.wait_ge(s_("turned"), g + 1)
                banks = [(u, b, min(PB, nt - PB * b)) for u in range(2) for b in range(2)]
                sums = lambda u, b, n: acc[u][:, b, 0:n * FW].rearrange("p (t f) -> p t f", f=FW)
                for u, b, n in banks:
                    eng.tensor_scalar(den[:, u, PB * b:PB * b + n], sums(u, b, n)[:, :, HD], 1e-37, None, ALU.max)\
                       .then_inc(s_("dn"), 1)
                eng.wait_ge(s_("dn"), 5 * g + 4)
                eng.reciprocal(rden[:, :, 0:nt], den[:, :, 0:nt]).then_inc(s_("dn"), 1)
                eng.wait_ge(s_("dn"), 5 * g + 5)
                for u, b, n in banks:
                    t = t0 + PB * b
                    eng.tensor_tensor(o[:, t:t + n, bass.ds(2 * HD * i + HD * u, HD)], sums(u, b, n)[:, :, 0:HD],
                                      rden[:, u, PB * b:PB * b + n].unsqueeze(2).to_broadcast([P, n, HD]), ALU.mult)\
                       .then_inc(s_("o"), 1)
                eng.wait_ge(s_("o"), 4 * g + 4)
                eng.sem_inc(s_("ev"), 1)
            passes(eng, count, after=divide)

        @block.tensor
        def _(eng):
            eng.sem_inc(s_("m"), 4)

            def sums(i, half, g, k, s, r):
                first = isinstance(k, int)
                cols = halves[half][1] * P
                if first:
                    eng.wait_ge(s_("ev"), g + 1)
                eng.wait_ge(s_("ft"), NT * g + k + 1)
                for u in range(2):
                    eng.wait_ge(s_("w"), 2 * NT * g + 2 * k + u + 3)
                    for b, c in enumerate(range(0, cols, BANK)):
                        n = min(BANK, cols - c)
                        last = eng.matmul(acc[u][0:FW, b, 0:n], ft[:, s, u, :], wgt[:, s, u, c:c + n],
                                          start=first, stop=True, skip_group_check=True)
                    last.then_inc(s_("m"), 1)

            def turn(i, half, g):
                eng.wait_ge(s_("oT"), 2 * g + 2)
                for u in range(2):
                    for t in range(halves[half][1]):
                        last = eng.transpose(acc[u][:, t // PB, (t % PB) * FW:(t % PB + 1) * FW],
                                             oT[0:FW, u, t * P:(t + 1) * P], ident[0:FW, 0:FW])
                last.then_inc(s_("turned"), 1)
            passes(eng, sums, after=turn)


def l3_tail(nc, sem, sb, a, out):
    xs, o = a.xs, a.hx[:, :, 0:D]
    s_ = lambda n: sem("l3t_" + n)
    with ExitStack() as ctx:
        neg = sb("neg", [P, NT, D], F32, ctx)
        block = ctx.enter_context(nc.Block())
        parts = [slice(5 * c, 5 * c + 5) for c in range(NT // 5)]

        @block.vector
        def _(eng):
            def finish(c):
                t = parts[c]
                eng.wait_ge(s_("elu"), c + 1)
                eng.wait_ge(s_("pos"), c + 1)
                eng.scalar_tensor_tensor(out=xs[:, t, :], in0=neg[:, t, :], scalar=-1.0, in1=xs[:, t, :],
                                         op0=ALU.add, op1=ALU.add).then_inc(s_("x"), 1)
            for c, t in enumerate(parts):
                eng.tensor_scalar(neg[:, t, :], o[:, t, :], 0.0, None, ALU.min).then_inc(s_("neg"), 1)
                eng.scalar_tensor_tensor(out=xs[:, t, :], in0=o[:, t, :], scalar=0.0, in1=xs[:, t, :],
                                         op0=ALU.max, op1=ALU.add).then_inc(s_("pos"), 1)
                if c:
                    finish(c - 1)
            finish(len(parts) - 1)

        @block.scalar
        def _(eng):
            for c, t in enumerate(parts):
                eng.wait_ge(s_("neg"), c + 1)
                eng.activation(neg[:, t, :], neg[:, t, :], ACT.Exp).then_inc(s_("elu"), 1)

        @block.sync
        def _(eng):
            full = lambda t0, t1: eng.dma_start(out[t0 * P:t1 * P, :].rearrange("(t p) d -> p t d", p=P), xs[:, t0:t1, :])
            for c, t in enumerate(parts):
                eng.wait_ge(s_("x"), c + 1)
                full(t.start, min(t.stop, NT - 1)).then_inc(s_("out"), 16)
            eng.dma_start(out[(NT - 1) * P:N, :], xs[0:N - (NT - 1) * P, NT - 1, :]).then_inc(s_("out"), 16)
            eng.wait_ge(s_("out"), 16 * (len(parts) + 1))


def l3_general(nc, sem, sb, a, ftx, sc, sc02, rr):
    psum, hx, ident = a.psum, a.hx, a.ident
    rows = nc.dram_tensor("rows", [2 * H, NP], F32)
    rrows = nc.dram_tensor("rrows", [2 * H, NP], F32)
    s_ = lambda n: sem("l3g_" + n)
    flat2 = lambda t: t.rearrange("p a d -> p (a d)")
    with ExitStack() as ctx:
        def buf(name, shape, dt=F32):
            return sb(name, shape, dt, ctx)
        a1 = buf("a1", [P, H, NP])
        cm = buf("cm", [P, 2, NT, P])
        mb = buf("mb", [P, 2, NP])
        junk = buf("junk", [P, NP], BF16)
        mx = buf("mx", [P, 2, H])
        top = buf("top", [P, NT, H])
        x1, x2, some = buf("x1", [P, NT, H]), buf("x2", [P, NT, H]), buf("some", [P, NT, H])
        rsb = buf("rsb", [2 * H, NP])
        pR = psum[:, 4:6, :]
        block = ctx.enter_context(nc.Block())

        @block.sync
        def _(eng):
            eng.wait_ge(s_("rtook"), 2 + 7)
            eng.dma_start(rows.ap(), rsb[:, :]).then_inc(s_("rows"), 16)
            eng.wait_ge(s_("rows"), 16)
            for h in range(H):
                eng.dma_start(a1[:, h, :], rows.ap()[h:h + 1, :].to_broadcast([P, NP])).then_inc(s_("a1"), 16)

            def load(k, s, r):
                if not isinstance(k, int):
                    eng.wait_ge(s_("mb"), k)
                eng.dma_start(cm[:, s, :, :], a.counts_t.ap()[:, :, bass.ds(k, 1), :].rearrange("j p k s -> p (j k) s"))\
                   .then_inc(s_(f"cm{s}"), 16)
            skewed(eng, NT, load)
            eng.wait_ge(s_("r2took"), 2 + 7)
            eng.dma_start(rrows.ap(), rsb[:, :]).then_inc(s_("rrows"), 16)
            eng.wait_ge(s_("rrows"), 16)

        @block.gpsimd
        def _(eng):
            eng.sem_inc(s_("mb"), 1)

            def mask(k, s, r):
                eng.wait_ge(s_(f"cm{s}"), 16 * r + 16)
                eng.wait_ge(s_("top"), k + 1)
                eng.sem_inc(s_("pass"), 1)
                eng.tensor_scalar(mb[:, s, :], cm[:, s, :, :].rearrange("p j s -> p (j s)"), 0.0, -BIG,
                                  ALU.is_equal, ALU.mult).then_inc(s_("mb"), 1)
            skewed(eng, NT, mask)

        @block.vector
        def _(eng):
            eng.sem_inc(s_("top"), 2)
            take_rows(eng, rsb, pR, s_("rready"), s_("rtook"))
            eng.wait_ge(s_("a1"), 64)

            def reduce(k, s, r):
                eng.wait_ge(s_("mb"), k + 2)
                if not isinstance(k, int):
                    eng.wait_ge(s_("top"), k + 1)
                eng.sem_inc(s_("pass"), 1)
                for h in range(H):
                    eng.tensor_tensor_reduce(out=junk[:, :], in0=mb[:, s, :], in1=a1[:, h, :], scale=1.0, scalar=-BIG,
                                             op0=ALU.add, op1=ALU.max, accum_out=mx[:, s, h:h + 1]).then_inc(s_("head"), 1)
                    eng.wait_ge(s_("head"), H * k + h + 1)
                    eng.sem_inc(s_("pass"), 1)
                eng.tensor_copy(flat2(top[:, bass.ds(k, 1), :]), mx[:, s, :]).then_inc(s_("top"), 1)
            skewed(eng, NT, reduce)
            eng.wait_ge(s_("top"), NT + 2)
            ch = Chain(eng, s_("dve2"))
            do, after = ch.do, ch.after
            a2, a02 = sc[:, :, H:2 * H], sc02[:, :, H:2 * H]
            do(eng.tensor_tensor(x1[:, :, :], top[:, :, :], a2, ALU.add))
            do(eng.tensor_scalar(some[:, :, :], top[:, :, :], -0.5 * BIG, None, ALU.is_gt))
            after()
            do(eng.tensor_scalar(x2[:, :, :], x1[:, :, :], 0.2, None, ALU.mult))
            after()
            do(eng.tensor_tensor(x1[:, :, :], x1[:, :, :], x2[:, :, :], ALU.max))
            after()
            do(eng.tensor_tensor(x1[:, :, :], x1[:, :, :], some[:, :, :], ALU.mult))
            after()
            do(eng.tensor_tensor(rr[:, :, 0:H], a2, x1[:, :, :], ALU.subtract))
            do(eng.tensor_tensor(rr[:, :, H:2 * H], a02, x1[:, :, :], ALU.subtract))
            after()
            eng.sem_inc(s_("rr"), 1)
            take_rows(eng, rsb, pR, s_("r2ready"), s_("r2took"))

        @block.tensor
        def _(eng):
            to_rows(eng, sc, ident, pR, s_("rready"), s_("rtook"))
            eng.wait_ge(s_("rr"), 1)
            to_rows(eng, rr, ident, pR, s_("r2ready"), s_("r2took"))

    with ExitStack() as ctx:
        def buf(name, shape, dt=F32):
            return sb(name, shape, dt, ctx)
        rb = buf("rb", [P, 2, 2, NP])
        t4 = buf("t4", [P, 4, NP])
        cj = buf("cj", [P, 2, NT, P])
        den = buf("den", [P, NT])
        rden = buf("rden", [P, NT])
        o = hx[:, :, 0:D]
        block = ctx.enter_context(nc.Block())
        acc = [psum[:, 4 * u:4 * u + 4, :] for u in range(2)]

        def at_(u, k):
            return acc[u][:, k // PB, (k % PB) * FW:(k % PB + 1) * FW]

        @block.sync
        def _(eng):
            def head(h, u, i):
                eng.wait_ge(s_("ev"), h + 1)
                for n in range(2):
                    eng.dma_start(rb[:, u, n, :], rrows.ap()[bass.ds(H * n + h, 1), :].to_broadcast([P, NP]))\
                       .then_inc(s_(f"rb{u}"), 16)

                def load(cur, prev):
                    if cur:
                        k, s, half = cur
                        eng.wait_ge(s_("pm"), NT * h + k + (2 if isinstance(k, int) else 1))
                        eng.dma_start(cj[:, s % 2, :, :], a.counts.ap()[:, :, bass.ds(k, 1), :].rearrange("k p j d -> p (k j) d"))\
                           .then_inc(s_(f"cj{s % 2}"), 16)
                ring4(eng, load)
            heads(eng, head)

        @block.scalar
        def _(eng):
            def head(h, u, i):
                def step(cur, prev):
                    if cur:
                        k, s, half = cur
                        eng.wait_ge(s_(f"rb{u}"), 32 * i + 32)
                        eng.wait_ge(s_("mm"), NT * h + k + (4 if isinstance(k, int) else 1))
                        eng.activation(t4[:, s, :], rb[:, u, 0, :], ACT.Identity,
                                       bias=flat2(sc[:, bass.ds(k, 1), bass.ds(h, 1)])).then_inc(s_("t1"), 1)
                    if prev:
                        k, s, half = prev
                        eng.wait_ge(s_("mx"), NT * h + k + 1)
                        eng.activation(t4[:, s, :], t4[:, s, :], ACT.Exp).then_inc(s_("ex"), 1)
                ring4(eng, step)
            heads(eng, head)

        @block.vector
        def _(eng):
            eng.sem_inc(s_("ev"), 2)
            eng.sem_inc(s_("pm"), 2)

            def head(h, u, i):
                def step(cur, prev):
                    if cur:
                        k, s, half = cur
                        eng.wait_ge(s_("t1"), NT * h + k + 1)
                        eng.scalar_tensor_tensor(out=t4[:, s, :], in0=rb[:, u, 1, :],
                                                 scalar=flat2(sc02[:, bass.ds(k, 1), bass.ds(h, 1)]),
                                                 in1=t4[:, s, :], op0=ALU.add, op1=ALU.max).then_inc(s_("mx"), 1)
                    if prev:
                        k, s, half = prev
                        eng.wait_ge(s_("ex"), NT * h + k + 1)
                        loads = (NT - NT // 2, NT // 2)[s % 2]
                        eng.wait_ge(s_(f"cj{s % 2}"), 16 * (loads * h + half + 1))
                        eng.scalar_tensor_tensor(out=t4[:, s, :], in0=t4[:, s, :], scalar=1.0,
                                                 in1=cj[:, s % 2, :, :].rearrange("p k d -> p (k d)"),
                                                 op0=ALU.min, op1=ALU.mult).then_inc(s_("pm"), 1)
                ring4(eng, step)
                eng.wait_ge(s_("mm"), NT * h + NT + 4)
                for b in range(4):
                    n = min(PB, NT - PB * b)
                    av = acc[u][:, b, 0:n * FW].rearrange("p (t f) -> p t f", f=FW)
                    eng.tensor_scalar(den[:, PB * b:PB * b + n], av[:, :, HD], 1e-30, None, ALU.max).then_inc(s_("dn"), 1)
                eng.wait_ge(s_("dn"), 8 * h + 4)
                eng.reciprocal(rden[:, :], den[:, :]).then_inc(s_("dn"), 1)
                eng.wait_ge(s_("dn"), 8 * h + 5)
                for b in range(4):
                    n = min(PB, NT - PB * b)
                    av = acc[u][:, b, 0:n * FW].rearrange("p (t f) -> p t f", f=FW)
                    last = eng.tensor_tensor(o[:, PB * b:PB * b + n, bass.ds(HD * h, HD)], av[:, :, 0:HD],
                                             rden[:, PB * b:PB * b + n].unsqueeze(2).to_broadcast([P, n, HD]), ALU.mult)
                    last.then_inc(s_("ev"), 1) if b == 3 else last.then_inc(s_("dn"), 1)
                eng.wait_ge(s_("dn"), 8 * h + 8)
            heads(eng, head)

        @block.tensor
        def _(eng):
            eng.sem_inc(s_("mm"), 4)

            def head(h, u, i):
                def step(cur, prev):
                    if cur:
                        k, s, half = cur
                        if isinstance(k, int):
                            eng.wait_ge(s_("ev"), h + 1)
                        eng.wait_ge(s_("pm"), NT * h + k + 3)
                        for d in range(NT):
                            last = eng.matmul(at_(u, d), t4[:, s, d * P:(d + 1) * P],
                                              ftx[:, bass.ds(k, 1), bass.ds(h, 1), :].rearrange("p a h d -> p (a h d)"),
                                              start=isinstance(k, int) and d % PB == 0, stop=True, skip_group_check=True)
                        last.then_inc(s_("mm"), 1)
                ring4(eng, step)
            heads(eng, head)


def kernel(**inp):
    import numpy as np
    import concourse.bacc as bacc
    from concourse.bass_utils import run_bass_kernel_spmd as run
    nc = bacc.Bacc("TRN2", target_bir_lowering=False, num_devices=1)
    g = {k: np.asarray(v) for k, v in inp.items()}
    a = {}
    a["x"] = g["x"]
    a["src"] = np.concatenate([g["src"], np.full(EP - E, NP - 1, np.int32)])
    a["dst"] = np.concatenate([g["dst"], np.full(EP - E, NP - 1, np.int32), NP + np.arange(EC, dtype=np.int32)])
    a["ew"] = np.concatenate([g["edge_weight"], np.zeros(EP - E, np.float32)])
    a["iota"] = np.tile(np.arange(P, dtype=np.float32), (P, 1))
    a["group"] = (np.arange(EP) // (P * GS) + 1).astype(np.float32).reshape(P, EC)
    a["vecs"] = np.stack([g["L0_gnn_b"], g["L1_gnn_b2"], g["L2_gnn_b0"], g["L2_gnn_b1"], g["L2_gnn_gamma"],
                          g["L2_gnn_beta"], g["L3_gnn_attn_l"].reshape(D), g["L3_gnn_attn_r"].reshape(D)])
    a["cols"] = np.stack([g["L1_gnn_b"].reshape(2, P), g["L1_gnn_b1"].reshape(2, P)]).reshape(4, P).T.copy()
    a["w0"] = np.concatenate([g["L0_gnn_W1"], g["L0_gnn_W2"]])
    a["w1"] = np.concatenate([g["L1_gnn_W"], g["L1_gnn_W1"], g["L1_gnn_W2"]])
    a["w2"] = np.concatenate([g["L2_gnn_W0"].T, g["L2_gnn_W1"].T])
    a["w3"] = np.ascontiguousarray(g["L3_gnn_W"].T)
    args = [nc.dram_tensor("in_" + k, v.shape, mybir.dt.from_np(v.dtype), kind="ExternalInput").ap() for k, v in a.items()]
    out = nc.dram_tensor("out_0", (N, D), F32, kind="ExternalOutput").ap()
    build(nc, *args, out)
    r = run(nc, [{"in_" + k: v for k, v in a.items()}], core_ids=[0])
    return r.results[0]["out_0"]
```
